# Optimizing a Trainium2 kernel written in Bass

```python
import numpy as np
import jax
import jax.numpy as jnp

def _softmax(x, axis=-1):
    return jax.nn.softmax(x, axis=axis)

def _gelu(x):
    return jax.nn.gelu(x, approximate=True)

def _silu(x):
    return jax.nn.silu(x)

def _sigmoid(x):
    return jax.nn.sigmoid(x)

def _layernorm(x, axis=-1, eps=1e-05):
    m = jnp.mean(x, axis=axis, keepdims=True)
    v = jnp.var(x, axis=axis, keepdims=True)
    return (x - m) / jnp.sqrt(v + eps)

def _scatter_add(tgt, idx, src, axis=0):
    return tgt.at[idx].add(src)

def _segment_sum(src, seg, n):
    return jax.ops.segment_sum(src, seg, n)
kernel_name = 'mk_adj_preln_d2_adj_r2_8fb99b'

def setup_inputs(seed: int=0):
    np.random.seed(seed)
    _w = jnp.asarray

    def _rec_inputs():
        import jax
        import jax.numpy as jnp
        _gk = jax.random.key(seed)
        x = -0.0005963 + 1.001 * jax.random.normal(jax.random.fold_in(_gk, 1), (2048, 256), jnp.float32)
        _a = jax.random.bernoulli(jax.random.fold_in(_gk, 2), 0.0078125, (2048, 2048))
        _af = _a.astype(jnp.float32)
        adj = _af
        return (x, adj)
    x, adj = _rec_inputs()

    def _L0_gnn_setup():
        import jax, jax.numpy as jnp
        import numpy as np
        N = 3072
        D_IN = 256
        D_OUT = 256
        DENSITY = 0.005
        key = jax.random.key(seed)
        ks = jax.random.split(key, 12)
        x = jax.random.normal(ks[0], (N, D_IN), dtype=jnp.float32)
        adj_a = (jax.random.uniform(ks[1], (N, N)) < DENSITY).astype(jnp.float32)
        adj_b = (jax.random.uniform(ks[2], (N, N)) < DENSITY).astype(jnp.float32)
        W_sa = jax.random.normal(ks[3], (D_IN, D_OUT), dtype=jnp.float32) * (1.414 / np.sqrt(D_IN + D_OUT))
        a_sa = jax.random.normal(ks[4], (1, 2 * D_OUT), dtype=jnp.float32) * (1.414 / np.sqrt(1 + 2 * D_OUT))
        stdv = 1.0 / np.sqrt(D_OUT)
        W_gcnb = jax.random.uniform(ks[5], (D_IN, D_OUT), minval=-stdv, maxval=stdv, dtype=jnp.float32)
        b_gcnb = jax.random.uniform(ks[6], (D_OUT,), minval=-stdv, maxval=stdv, dtype=jnp.float32)
        s = 1.0 / np.sqrt(2 * D_IN)
        Wa = jax.random.uniform(ks[7], (1, 2 * D_IN), minval=-s, maxval=s, dtype=jnp.float32)
        ba = jax.random.uniform(ks[8], (1,), minval=-s, maxval=s, dtype=jnp.float32)
        Wb = jax.random.uniform(ks[9], (1, 2 * D_IN), minval=-s, maxval=s, dtype=jnp.float32)
        bb = jax.random.uniform(ks[10], (1,), minval=-s, maxval=s, dtype=jnp.float32)
        return {'x': x, 'adj_a': adj_a, 'adj_b': adj_b, 'W_sa': W_sa, 'a_sa': a_sa, 'W_gcnb': W_gcnb, 'b_gcnb': b_gcnb, 'Wa': Wa, 'ba': ba, 'Wb': Wb, 'bb': bb}
    _L0_gnn_all = _L0_gnn_setup()
    _L0_gnn_in = {k: v for k, v in _L0_gnn_all.items() if k in ('W_sa', 'a_sa', 'W_gcnb', 'b_gcnb', 'Wa', 'ba', 'Wb', 'bb')}
    del _L0_gnn_all

    def _L1_gnn_setup():
        import jax, jax.numpy as jnp
        import numpy as np
        N = 4096
        D_IN = 256
        D_OUT = 256
        NEG_BIG = -9000000000000000.0
        key = jax.random.key(seed)
        kx, ka, kw, kb, kn, ke = jax.random.split(key, 6)
        x = jax.random.normal(kx, (N, D_IN), dtype=jnp.float32)
        adj = (jax.random.uniform(ka, (N, N)) > 0.9).astype(jnp.float32)
        stdv = 1.0 / np.sqrt(D_OUT)
        weight = jax.random.uniform(kw, (D_IN, D_OUT), minval=-stdv, maxval=stdv, dtype=jnp.float32)
        bias = jax.random.uniform(kb, (D_OUT,), minval=-stdv, maxval=stdv, dtype=jnp.float32)
        node_w = jax.random.uniform(kn, (D_IN, 1), minval=-1.0, maxval=1.0, dtype=jnp.float32)
        stdv_e = 1.0 / np.sqrt(D_IN)
        edge_w = jax.random.uniform(ke, (D_IN, D_IN), minval=-stdv_e, maxval=stdv_e, dtype=jnp.float32)
        return {'x': x, 'adj': adj, 'weight': weight, 'bias': bias, 'node_w': node_w, 'edge_w': edge_w}
    _L1_gnn_all = _L1_gnn_setup()
    _L1_gnn_in = {k: v for k, v in _L1_gnn_all.items() if k in ('weight', 'bias', 'node_w', 'edge_w')}
    del _L1_gnn_all
    return {'x': x, 'adj': adj, 'L0_gnn_W_sa': _L0_gnn_in['W_sa'], 'L0_gnn_a_sa': _L0_gnn_in['a_sa'], 'L0_gnn_W_gcnb': _L0_gnn_in['W_gcnb'], 'L0_gnn_b_gcnb': _L0_gnn_in['b_gcnb'], 'L0_gnn_Wa': _L0_gnn_in['Wa'], 'L0_gnn_ba': _L0_gnn_in['ba'], 'L0_gnn_Wb': _L0_gnn_in['Wb'], 'L0_gnn_bb': _L0_gnn_in['bb'], 'L1_gnn_weight': _L1_gnn_in['weight'], 'L1_gnn_bias': _L1_gnn_in['bias'], 'L1_gnn_node_w': _L1_gnn_in['node_w'], 'L1_gnn_edge_w': _L1_gnn_in['edge_w']}

def reference(x, adj, L0_gnn_W_sa, L0_gnn_a_sa, L0_gnn_W_gcnb, L0_gnn_b_gcnb, L0_gnn_Wa, L0_gnn_ba, L0_gnn_Wb, L0_gnn_bb, L1_gnn_weight, L1_gnn_bias, L1_gnn_node_w, L1_gnn_edge_w):
    import jax
    import jax.numpy as jnp

    def _L0_gnn_ref(x, adj_a, adj_b, W_sa, a_sa, W_gcnb, b_gcnb, Wa, ba, Wb, bb):
        import jax, jax.numpy as jnp
        import numpy as np
        N = 3072
        D_IN = 256
        D_OUT = 256
        DENSITY = 0.005
        type_sum_a = adj_a @ x
        type_sum_b = adj_b @ x
        attn_a = jax.nn.sigmoid(jnp.concatenate([type_sum_a, x], axis=1) @ Wa.T + ba)
        attn_b = jax.nn.sigmoid(jnp.concatenate([type_sum_b, x], axis=1) @ Wb.T + bb)
        h = x @ W_sa
        Hd = h.shape[1]
        s_left = h @ a_sa[0, :Hd]
        s_right = h @ a_sa[0, Hd:]
        scores = s_left[:, None] + s_right[None, :]
        e = jnp.where(adj_a != 0, jnp.exp(-jax.nn.leaky_relu(scores, 0.01)), 0.0)
        attn = e / (jnp.sum(e, axis=1, keepdims=True) + 1e-05)
        x_a = attn @ h
        x_b = adj_b @ (x @ W_gcnb) + b_gcnb
        return jax.nn.sigmoid(attn_a * x_a + attn_b * x_b)

    def _L1_gnn_ref(x, adj, weight, bias, node_w, edge_w):
        import jax, jax.numpy as jnp
        import numpy as np
        N = 4096
        D_IN = 256
        D_OUT = 256
        NEG_BIG = -9000000000000000.0
        node_att = jax.nn.softmax(x @ node_w, axis=0)
        h = x @ edge_w
        e = h @ h.T
        e = jnp.where(adj > 0, e, NEG_BIG)
        edge_att = jax.nn.softmax(e, axis=1)
        combined_att = node_att * edge_att
        support = x @ weight
        output = adj * combined_att @ support
        return output + bias
    h = jnp.maximum(_layernorm(x, axis=-1), 0.0)
    x = x + _L0_gnn_ref(h, adj, adj, L0_gnn_W_sa, L0_gnn_a_sa, L0_gnn_W_gcnb, L0_gnn_b_gcnb, L0_gnn_Wa, L0_gnn_ba, L0_gnn_Wb, L0_gnn_bb)
    h = jnp.maximum(_layernorm(x, axis=-1), 0.0)
    x = x + _L1_gnn_ref(h, adj, L1_gnn_weight, L1_gnn_bias, L1_gnn_node_w, L1_gnn_edge_w)
    return x

_drawn_inputs = setup_inputs


def setup_inputs(seed=0):
    import zlib

    import numpy as np

    out = dict(_drawn_inputs(seed))
    spreads = {}
    factors = {'L0_gnn_W_sa': 3.599,
     'L0_gnn_a_sa': 61.982,
     'L0_gnn_b_gcnb': 26.481,
     'L0_gnn_Wa': 4.31,
     'L1_gnn_weight': 8.0,
     'L1_gnn_node_w': 8.0,
     'L1_gnn_edge_w': 8.0}
    for name, (base, spread) in spreads.items():
        noise = np.random.default_rng([zlib.crc32(name.encode()), seed]).standard_normal(out[name].shape)
        drawn = base * np.exp(spread * noise) if base else spread * noise
        out[name] = jnp.asarray(drawn.astype(out[name].dtype))
    for name, factor in factors.items():
        out[name] = (out[name] * factor).astype(out[name].dtype)
    return out
```

```python
import concourse.bass as bass
from concourse import mybir
from contextlib import ExitStack


def build_two_graph_blocks(nc: bass.Bass, x, adj, adj_t, W_sa, a_sa, W_gcnb, b_gcnb, Wa, ba, Wb, bb,
                           weight, bias, node_w, edge_w, out):
    f32, f32r = mybir.dt.float32, mybir.dt.float32r
    ALU = mybir.AluOpType
    ACT = mybir.ActivationFunctionType
    AX = mybir.AxisListType
    RED = bass.bass_isa.ReduceOp

    P = 128
    N, D = x.shape
    KD = D // P
    NT = N // P
    GT = 4
    GN = GT * P
    NG = N // GN
    PAIRS = NT // 2
    EW = 4
    ER = 4
    DX = D + 2
    SLOPE = 0.01
    NEG_BIG = 9.0e15
    F32_MAX = 3.0e38
    EPS_LN, EPS_ATT = 1e-5, 1e-5

    ctx = ExitStack()
    with ctx:
        def sb(name, shape, dt=f32, on=ctx):
            return on.enter_context(nc.sbuf_tensor(name, shape, dt))

        def sem(name):
            return ctx.enter_context(nc.semaphore(name))

        x_sb = sb("x_sb", [P, NT, D])
        z_sb = sb("z_sb", [P, 2, GT, D])
        stage_hi = sb("stage_hi", [P, 2, KD, GN], f32r)
        stage_lo = sb("stage_lo", [P, 2, KD, GN], f32r)
        ident = sb("ident", [P, P])
        stats = sb("stats", [P, NT, 6])
        mean_var = sb("mean_var", [P, NT, 2])
        var_eps = sb("var_eps", [P, NT])
        rstd = sb("rstd", [P, NT])
        minus_half = sb("minus_half", [P, NT])
        w1_raw = sb("w1_raw", [P, KD, 2 * D + 2])
        bgc_bc = sb("bgc_bc", [P, D])
        bias_bc = sb("bias_bc", [P, D])
        gate_bias = sb("gate_bias", [P, 2])
        wait_cell = sb("wait_cell", [P, 1])

        l0 = ExitStack()
        with l0:
            ab_hi = sb("ab_hi", [P, NT, 2, DX], f32r, l0)
            ab_lo = sb("ab_lo", [P, NT, 2, DX], f32r, l0)
            adj_ring = sb("adj_ring", [P, NT, GN], f32r, l0)
            e_hi = sb("e_hi", [P, ER, 2, GN], f32r, l0)
            e_lo = sb("e_lo", [P, ER, 2, GN], f32r, l0)
            sl_bc = sb("sl_bc", [P, N], f32, l0)
            extras = sb("extras", [P, NT, 6], f32, l0)
            gate_x = sb("gate_x", [P, NT, 2], f32, l0)
            gate_z = sb("gate_z", [P, GT, 2], f32, l0)
            gate_t = sb("gate_t", [P, GT, 2], f32, l0)
            gate = sb("gate", [P, GT, 2], f32, l0)
            mv_block = sb("mv_block", [P, GT, 2], f32, l0)
            e_sum = sb("e_sum", [P, GT], f32, l0)
            e_rsum = sb("e_rsum", [P, GT], f32, l0)
            coef_a = sb("coef_a", [P, GT], f32, l0)
            yb, y_t = z_sb[:, 0, :, :], z_sb[:, 1, :, :]
            w0 = ExitStack()
            with w0:
                w0_raw = sb("w0_raw", [P, KD, 2 * D], f32, w0)
                a_bc = sb("a_bc", [P, 2 * D], f32, w0)
                w0_hi = sb("w0_hi", [P, KD, 2 * D], f32r, w0)
                w0_lo = sb("w0_lo", [P, KD, 2 * D], f32r, w0)
                xc_raw = sb("xc_raw", [P, KD, 6], f32, w0)
                xc_hi = sb("xc_hi", [P, KD, 6], f32r, w0)
                xc_lo = sb("xc_lo", [P, KD, 6], f32r, w0)
                u_left = sb("u_left", [P, KD], f32, w0)
                ul_hi = sb("ul_hi", [P, KD, P], f32r, w0)
                ul_lo = sb("ul_lo", [P, KD, P], f32r, w0)
                u_junk = sb("u_junk", [P, 2, D], f32, w0)
            ew = sb("ew", [P, EW, 2, GN], f32, l0)

        hh_hi = sb("hh_hi", [P, KD, N], f32r)
        hh_lo = sb("hh_lo", [P, KD, N], f32r)
        s_hi = sb("s_hi", [P, NT, D], f32r)
        s_lo = sb("s_lo", [P, NT, D], f32r)
        w1_hi = sb("w1_hi", [P, KD, 2 * D + 2], f32r)
        w1_lo = sb("w1_lo", [P, KD, 2 * D + 2], f32r)
        mask = sb("mask", [P, 2, N])
        em = sb("em", [P, 2, N])
        pt_hi = sb("pt_hi", [P, 2, NT, P], f32r)
        pt_lo = sb("pt_lo", [P, 2, NT, P], f32r)
        hs_hi = sb("hs_hi", [P, 2, KD, P], f32r)
        hs_lo = sb("hs_lo", [P, 2, KD, P], f32r)
        row_max2 = sb("row_max2", [P, 2, 2])
        neg_max = sb("neg_max", [P, 2])
        row_sum = sb("row_sum", [P, 2])
        row_rsum = sb("row_rsum", [P, 2])
        row_flag = sb("row_flag", [P, 2])
        row_coef = sb("row_coef", [P, 2])
        o_sb = sb("o_sb", [P, 2, D])
        v_sb = sb("v_sb", [P, NT])
        v_max = sb("v_max", [P, 1])
        v_gmax = sb("v_gmax", [P, 1])
        v_ngmax = sb("v_ngmax", [P, 1])
        v_exp = sb("v_exp", [P, NT])
        v_sum = sb("v_sum", [P, 1])
        v_gsum = sb("v_gsum", [P, 1])
        v_rsum = sb("v_rsum", [P, 1])
        node_att = sb("node_att", [P, NT])

        ps = ctx.enter_context(nc.psum_tensor("ps", [P, 8, GN], f32))

        x_loaded = [sem(f"x_loaded{g}") for g in range(NG)]
        w0_loaded, w1_loaded, vec_loaded = sem("w0_loaded"), sem("w1_loaded"), sem("vec_loaded")
        consts_ready = sem("consts_ready")
        ident_z = sem("ident_z")
        stats_d = sem("stats_d")
        mv_ready = sem("mv_ready")
        ve_ready = sem("ve_ready")
        rstd_ready = sem("rstd_ready")
        u_ready, wsplit_hi, wsplit = sem("u_ready"), sem("wsplit_hi"), sem("wsplit")
        z_ready = sem("z_ready")
        tr_done = sem("tr_done")
        sthi_ready, stlo_ready = sem("sthi_ready"), sem("stlo_ready")
        stage_used = sem("stage_used")
        g_done, g_hi, g_lo = sem("g_done"), sem("g_hi"), sem("g_lo")
        sl_done, sl_ready = sem("sl_done"), sem("sl_ready")
        exs_ready, ab_ready = sem("exs_ready"), sem("ab_ready")
        abx_hi = sem("abx_hi")
        adj_loaded = [sem(f"adj_loaded{g}") for g in range(4)]
        adj_pe = sem("adj_pe")
        ew_s, ew_z, ew_x, ew_m = sem("ew_s"), sem("ew_z"), sem("ew_x"), sem("ew_m")
        ehi_ready = sem("ehi_ready")
        elo_ready = sem("elo_ready")
        e_used = sem("e_used")
        xb_free, xa_free = sem("xb_free"), sem("xa_free")
        gz_ready, gt_ready, gate_ready = sem("gz_ready"), sem("gt_ready"), sem("gate_ready")
        yb_ready, esum_ready, ersum_ready, coef_ready = (sem("yb_ready"), sem("esum_ready"),
                                                         sem("ersum_ready"), sem("coef_ready"))
        ybs_ready, yt_ready, yh_ready, x1_ready = sem("ybs_ready"), sem("yt_ready"), sem("yh_ready"), sem("x1_ready")
        x1_kept, mvb_ready = sem("x1_kept"), sem("mvb_ready")
        w1_hi_s, w1_s = sem("w1_hi_s"), sem("w1_s")
        xbias_ready = sem("xbias_ready")
        h1_done, h1_hi, h1_lo = sem("h1_done"), sem("h1_hi"), sem("h1_lo")
        s1_done, s1_hi, s1_lo, v_ready = sem("s1_done"), sem("s1_hi"), sem("s1_lo"), sem("v_ready")
        vmax_s, vgmax_s, vneg_s, vexp_s, vgsum_s, vr_s, natt_ready = (
            sem("vmax_s"), sem("vgmax_s"), sem("vneg_s"), sem("vexp_s"), sem("vgsum_s"), sem("vr_s"),
            sem("natt_ready"))
        mask_loaded = [sem("mask_loaded0"), sem("mask_loaded1")]
        mask_ready = sem("mask_ready")
        hs_ready = sem("hs_ready")
        e_done = sem("e_done")
        em_ready = sem("em_ready")
        nmax_ready, p_ready = sem("nmax_ready"), sem("p_ready")
        t_done = sem("t_done")
        pthi_ready, ptlo_ready = sem("pthi_ready"), sem("ptlo_ready")
        o_done, o_ready = sem("o_done"), sem("o_ready")
        rr_ready, rf_ready, rc_ready = sem("rr_ready"), sem("rf_ready"), sem("rc_ready")
        out_stored = [sem("out_stored0"), sem("out_stored1")]

        xg = x.rearrange("(g t p) d -> g p t d", t=GT, p=P)
        adjt_v = adj_t.rearrange("(q t p) n -> q p t n", q=4, p=P)
        adj_v = adj.rearrange("(t p) n -> t p n", p=P)
        out_v = out.rearrange("(t p) d -> t p d", p=P)

        def kview(w):
            return w.rearrange("(k p) c -> p k c", p=P)

        def three_products(pe_out, lhs_hi, lhs_lo, rhs_hi, rhs_lo):
            terms = [(lhs_hi, rhs_hi), (lhs_hi, rhs_lo), (lhs_lo, rhs_hi)]
            for n, (a, b) in enumerate(terms):
                for k in range(KD):
                    last = nc.tensor.matmul(pe_out, a(k), b(k), start=(n == 0 and k == 0),
                                            stop=(n == 2 and k == KD - 1))
            return last

        block = ctx.enter_context(nc.Block())

        @block.sync
        def _(sp):
            for g in range(NG):
                sp.dma_start(x_sb[:, g * GT:(g + 1) * GT, :], xg[g]).then_inc(x_loaded[g], 16)
                if g == 0:
                    sp.dma_start(w0_raw[:, :, 0:D], kview(W_sa)).then_inc(w0_loaded, 16)
                    sp.dma_start(w0_raw[:, :, D:2 * D], kview(W_gcnb)).then_inc(w0_loaded, 16)
            sp.dma_start(a_bc[:, :], a_sa[0].partition_broadcast(P)).then_inc(w0_loaded, 16)
            for c, w in ((1, Wa), (2, Wb)):
                for side in range(2):
                    sp.dma_start(xc_raw[:, :, c + 2 * side:c + 2 * side + 1],
                                 w[0:1, side * D:(side + 1) * D].rearrange("o (k p) -> p k o", p=P),
                                 allow_slow_non_contiguous=True).then_inc(w0_loaded, 16)
            sp.dma_start(bgc_bc[:, :], b_gcnb.partition_broadcast(P)).then_inc(vec_loaded, 16)
            sp.dma_start(bias_bc[:, :], bias.partition_broadcast(P)).then_inc(vec_loaded, 16)
            sp.dma_start(gate_bias[:, 0:1], ba.partition_broadcast(P)).then_inc(vec_loaded, 16)
            sp.dma_start(gate_bias[:, 1:2], bb.partition_broadcast(P)).then_inc(vec_loaded, 16)
            sp.dma_start(w1_raw[:, :, 0:D], kview(edge_w)).then_inc(w1_loaded, 16)
            sp.dma_start(w1_raw[:, :, D:2 * D], kview(weight)).then_inc(w1_loaded, 16)
            sp.dma_start(w1_raw[:, :, 2 * D:2 * D + 1], kview(node_w),
                         allow_slow_non_contiguous=True).then_inc(w1_loaded, 16)

            sp.wait_ge(e_used, ER + NG * PAIRS)
            sp.wait_ge(x1_kept, NG)
            for t in range(2):
                sp.dma_start(mask[:, t, :], adj_v[t]).then_inc(mask_loaded[t], 16)
            with sp.Fori(0, NT // 2 - 1) as i:
                for s in range(2):
                    sp.wait_ge(em_ready, i * 4 + 2 * s + 2)
                    sp.dma_start(mask[:, s, :], adj_v[i * 2 + s + 2]).then_inc(mask_loaded[s], 16)
                for s in range(2):
                    sp.wait_ge(o_ready, i * 2 + s + 1)
                    sp.dma_start(out_v[i * 2 + s], o_sb[:, s, :]).then_inc(out_stored[s], 16)
            for s in range(2):
                sp.wait_ge(o_ready, NT - 1 + s)
                sp.dma_start(out_v[NT - 2 + s], o_sb[:, s, :]).then_inc(out_stored[s], 16)
            for s in range(2):
                sp.wait_ge(out_stored[s], 16 * (NT // 2))

        @block.gpsimd
        def _(pool):
            def load_adj_quarter(b, q):
                pool.dma_start(adj_ring[:, q * 4:(q + 1) * 4, :],
                               adjt_v[q][:, :, bass.ds(b * GN, GN)]).then_inc(adj_loaded[q], 16)

            nc.gpsimd.memset(ident[:, :], 0.0).then_inc(ident_z, 1)
            nc.gpsimd.memset(minus_half[:, :], -0.5)
            nc.gpsimd.memset(xc_raw[:, :, 5:6], 0.0)
            nc.gpsimd.memset(w1_raw[:, :, 2 * D + 1:2 * D + 2], 0.0)
            pool.wait_ge(ident_z, 1)
            nc.gpsimd.affine_select(out=ident[:, :], in_=ident[:, :], compare_op=ALU.not_equal, fill=1.0, base=0,
                                    pattern=[[-1, P]], channel_multiplier=1).then_inc(consts_ready, 1)
            for g in range(NG):
                pool.wait_ge(mv_ready, GT * (g + 1))
                sl = slice(g * GT, (g + 1) * GT)
                nc.gpsimd.tensor_scalar(var_eps[:, sl], mean_var[:, sl, 1], EPS_LN, None, ALU.add
                                        ).then_inc(ve_ready, 1)
                pool.wait_ge(ve_ready, g + 1)
                nc.gpsimd.tensor_tensor(var_eps[:, sl], var_eps[:, sl], minus_half[:, sl], ALU.pow
                                        ).then_inc(rstd_ready, 1)
            for q in range(4):
                load_adj_quarter(0, q)
            with pool.Fori(1, NG) as b:
                for q in range(4):
                    pool.wait_ge(adj_pe, b * 4 + (q + 1 - 4))
                    pool.wait_ge(ew_m, b * PAIRS + (2 * q + 2 - PAIRS))
                    load_adj_quarter(b, q)
            pool.wait_ge(mv_ready, 2 * NT)
            nc.gpsimd.tensor_scalar(rstd[:, :], mean_var[:, :, 1], EPS_LN, None, ALU.add).then_inc(ve_ready, 1)
            pool.wait_ge(ve_ready, NG + 1)
            nc.gpsimd.tensor_tensor(rstd[:, :], rstd[:, :], minus_half[:, :], ALU.pow).then_inc(rstd_ready, 1)
            pool.wait_ge(vmax_s, 1)
            nc.gpsimd.partition_all_reduce(v_gmax[:, :], v_max[:, :], P, RED.max).then_inc(vgmax_s, 1)
            def stage_row(i, s):
                nc.gpsimd.tensor_copy(hs_hi[:, s, :, :], hh_hi[:, :, bass.ds(i * P, P)].bitcast(f32))
                nc.gpsimd.tensor_copy(hs_lo[:, s, :, :], hh_lo[:, :, bass.ds(i * P, P)].bitcast(f32)
                                      ).then_inc(hs_ready, 1)
            pool.wait_ge(h1_hi, 2 * NG)
            pool.wait_ge(h1_lo, 2 * NG)
            stage_row(0, 0)
            stage_row(1, 1)
            pool.wait_ge(vexp_s, 1)
            nc.gpsimd.partition_all_reduce(v_gsum[:, :], v_sum[:, :], P, RED.add).then_inc(vgsum_s, 1)
            with pool.Fori(1, NT // 2) as i:
                for s in range(2):
                    pool.wait_ge(e_done, i * 4 + (2 * s + 2 - 4))
                    stage_row(i * 2 + s, s)

        @block.scalar
        def _(act):
            def relu_stage(n):
                act.wait_ge(tr_done, n + 1)
                if 2 <= n < NG + 2:
                    act.wait_ge(stage_used, min(n - 1, NG))
                if n >= NG + 2:
                    act.wait_ge(s1_done, GT * (n - NG - 1))
                nc.scalar.activation(stage_hi[:, n % 2, :, :], ps[:, 0:2, :], ACT.Relu).then_inc(sthi_ready, 1)

            for g in range(NG):
                relu_stage(g)
                for t in range(GT):
                    j = g * GT + t
                    act.wait_ge(g_done, j + 1)
                    nc.scalar.copy(ab_hi[:, j, :, 0:D], ps[:, 2 + j % 3, :].rearrange("p (c d) -> p c d", c=2)
                                   ).then_inc(g_hi, 1)
                act.wait_ge(sl_done, g + 1)
                nc.scalar.copy(sl_bc[:, g * GN:(g + 1) * GN], ps[:, 6 + g % 2, :]).then_inc(sl_ready, 1)

            act.wait_ge(exs_ready, 1)
            act.wait_ge(sl_ready, NG)
            with act.Fori(0, NG) as b:
                for step in range(PAIRS + 2):
                    if EW <= step < PAIRS:
                        act.wait_ge(elo_ready, b * PAIRS + step + 1)
                    if 0 <= step - 1 < PAIRS:
                        p = step - 1
                        act.wait_ge(ew_z, b * PAIRS + p + 1)
                        nc.scalar.activation(ew[:, p % EW, :, :], ew[:, p % EW, :, :], ACT.Exp, scale=-1.0
                                             ).then_inc(ew_x, 1)
                    if step < PAIRS:
                        p = step
                        for h in range(2):
                            j = 2 * p + h
                            last = nc.scalar.activation(ew[:, p % EW, h, :], sl_bc[:, bass.ds(b * GN, GN)],
                                                        ACT.Identity, bias=extras[:, j, 0:1])
                        last.then_inc(ew_s, 1)
                    if 0 <= step - 2 < PAIRS:
                        p = step - 2
                        act.wait_ge(ew_m, b * PAIRS + p + 1)
                        act.wait_ge(e_used, b * PAIRS + p + 1)
                        nc.scalar.copy(e_hi[:, p % ER, :, :], ew[:, p % EW, :, :]).then_inc(ehi_ready, 1)
                    if step == 6:
                        act.wait_ge(gz_ready, b + 1)
                        nc.scalar.activation(gate_t[:, :, :], gate_z[:, :, :], ACT.Tanh, scale=0.5
                                             ).then_inc(gt_ready, 1)
                act.wait_ge(xa_free, b + 2)
                nc.scalar.activation(y_t[:, :, :], yb[:, :, :], ACT.Tanh, scale=0.5).then_inc(yt_ready, 1)

            for g in range(NG):
                relu_stage(NG + g)
                for m in range(KD):
                    n = g * KD + m
                    act.wait_ge(h1_done, n + 1)
                    nc.scalar.copy(hh_hi[:, m, g * GN:(g + 1) * GN], ps[:, 2 + m, :]).then_inc(h1_hi, 1)
                for t in range(GT):
                    j = g * GT + t
                    act.wait_ge(s1_done, j + 1)
                    nc.scalar.copy(s_hi[:, j, :], ps[:, 4 + t, 0:D]).then_inc(s1_hi, 1)

            def make_mask(s, n):
                act.wait_ge(mask_loaded[s], n)
                nc.scalar.activation(mask[:, s, :], mask[:, s, :], ACT.Copy, bias=-NEG_BIG, scale=NEG_BIG
                                     ).then_inc(mask_ready, 1)

            def exp_row(i, s):
                act.wait_ge(nmax_ready, i + 1)
                nc.scalar.activation(em[:, s, :], em[:, s, :], ACT.Exp, bias=neg_max[:, s:s + 1],
                                     accum_out=row_sum[:, s:s + 1]).then_inc(p_ready, 1)

            def transposed_hi(i, s, q):
                act.wait_ge(t_done, i * 4 + q + 1)
                nc.scalar.copy(pt_hi[:, s, 4 * q:4 * q + 4, :],
                               ps[:, 4 + q % 2, :].rearrange("p (t c) -> p t c", t=4)).then_inc(pthi_ready, 1)

            make_mask(0, 16)
            make_mask(1, 16)
            act.wait_ge(vneg_s, 1)
            nc.scalar.activation(v_exp[:, :], v_sb[:, :], ACT.Exp, bias=v_ngmax[:, 0:1],
                                 accum_out=v_sum[:, :]).then_inc(vexp_s, 1)
            exp_row(0, 0)
            with act.Fori(0, NT // 2 - 1) as i:
                for s in range(2):
                    for q in range(4):
                        transposed_hi(i * 2 + s, s, q)
                    make_mask(s, i * 16 + 32)
                    exp_row(i * 2 + s + 1, 1 - s)
            for s in range(2):
                for q in range(4):
                    transposed_hi(NT - 2 + s, s, q)
                if s == 0:
                    exp_row(NT - 1, 1)

        @block.vector
        def _(dve):
            dve.sem_inc(elo_ready, EW)
            dve.sem_inc(e_used, ER)
            dve.sem_inc(xb_free, 1)
            dve.sem_inc(xa_free, 1)
            nc.vector.memset(ab_hi[:, :, 0, D:D + 1].bitcast(f32), 1.0)
            nc.vector.memset(ab_hi[:, :, 0, D + 1:D + 2].bitcast(f32), 0.0)

            def tile_stats(j, src, n):
                nc.vector.bn_stats(stats[:, j, :], src).then_inc(stats_d, 1)
                dve.wait_ge(stats_d, n + 1)
                nc.vector.bn_aggr(mean_var[:, j, :], stats[:, j, :]).then_inc(mv_ready, 1)

            def normalise(n, rs):
                g = n % NG
                if n >= 2:
                    dve.wait_ge(tr_done, n - 1)
                for t in range(GT):
                    j = g * GT + t
                    last = nc.vector.tensor_scalar(z_sb[:, n % 2, t, :], x_sb[:, j, :], mean_var[:, j, 0:1],
                                                   rs[:, j:j + 1], ALU.subtract, ALU.mult)
                last.then_inc(z_ready, 1)

            def relu_stage_lo(n):
                dve.wait_ge(sthi_ready, n + 1)
                nc.vector.scalar_tensor_tensor(out=stage_lo[:, n % 2, :, :], in0=ps[:, 0:2, :], scalar=0.0,
                                               in1=stage_hi[:, n % 2, :, :].bitcast(f32), op0=ALU.max,
                                               op1=ALU.subtract).then_inc(stlo_ready, 1)

            for g in range(NG):
                dve.wait_ge(x_loaded[g], 16)
                for t in range(GT):
                    j = g * GT + t
                    tile_stats(j, x_sb[:, j, :], j)
                if g == 0:
                    dve.wait_ge(w0_loaded, 7 * 16)
                    for k in range(KD):
                        nc.vector.tensor_tensor_reduce(out=u_junk[:, 0, :], in0=w0_raw[:, k, 0:D], in1=a_bc[:, 0:D],
                                                       scale=1.0, scalar=0.0, op0=ALU.mult, op1=ALU.add,
                                                       accum_out=u_left[:, k:k + 1]).then_inc(u_ready, 1)
                        dve.wait_ge(u_ready, 2 * k + 1)
                        nc.vector.tensor_tensor_reduce(out=u_junk[:, 1, :], in0=w0_raw[:, k, 0:D],
                                                       in1=a_bc[:, D:2 * D], scale=1.0, scalar=0.0, op0=ALU.mult,
                                                       op1=ALU.add, accum_out=xc_raw[:, k, 0:1]).then_inc(u_ready, 1)
                        dve.wait_ge(u_ready, 2 * k + 2)
                    dve.wait_ge(consts_ready, 1)
                    ul_b = u_left[:, :].unsqueeze(2).broadcast_to([P, KD, P])
                    nc.vector.tensor_copy(w0_hi[:, :, :], w0_raw[:, :, :])
                    nc.vector.tensor_copy(xc_hi[:, :, :], xc_raw[:, :, :])
                    nc.vector.tensor_copy(ul_hi[:, :, :], ul_b).then_inc(wsplit_hi, 1)
                    dve.wait_ge(wsplit_hi, 1)
                    nc.vector.tensor_tensor(w0_lo[:, :, :], w0_raw[:, :, :], w0_hi[:, :, :].bitcast(f32), ALU.subtract)
                    nc.vector.tensor_tensor(xc_lo[:, :, :], xc_raw[:, :, :], xc_hi[:, :, :].bitcast(f32), ALU.subtract)
                    nc.vector.tensor_tensor(ul_lo[:, :, :], ul_b, ul_hi[:, :, :].bitcast(f32), ALU.subtract
                                            ).then_inc(wsplit, 1)
                if g < 2:
                    dve.wait_ge(rstd_ready, g + 1)
                    normalise(g, var_eps)

            for g in range(NG):
                relu_stage_lo(g)
                for t in range(GT):
                    j = g * GT + t
                    dve.wait_ge(g_hi, j + 1)
                    nc.vector.tensor_tensor(ab_lo[:, j, :, 0:D],
                                            ps[:, 2 + j % 3, :].rearrange("p (c d) -> p c d", c=2),
                                            ab_hi[:, j, :, 0:D].bitcast(f32), ALU.subtract).then_inc(g_lo, 1)
                if g + 2 < NG:
                    dve.wait_ge(rstd_ready, g + 3)
                    normalise(g + 2, var_eps)

            dve.wait_ge(stage_used, NG)
            nc.vector.tensor_copy(extras[:, :, :], ps[:, 5, 0:NT * 6].rearrange("p (t c) -> p t c", c=6)
                                  ).then_inc(exs_ready, 1)
            dve.wait_ge(exs_ready, 1)
            nc.vector.tensor_copy(ab_hi[:, :, 1, D:DX], extras[:, :, 1:3]).then_inc(abx_hi, 1)
            dve.wait_ge(abx_hi, 1)
            nc.vector.tensor_tensor(ab_lo[:, :, 1, D:DX], extras[:, :, 1:3], ab_hi[:, :, 1, D:DX].bitcast(f32),
                                    ALU.subtract).then_inc(ab_ready, 1)
            dve.wait_ge(vec_loaded, 64)
            nc.vector.tensor_tensor(gate_x[:, :, :], extras[:, :, 3:5],
                                    gate_bias[:, :].unsqueeze(1).broadcast_to([P, NT, 2]), ALU.add
                                    ).then_inc(ab_ready, 1)
            dve.wait_ge(ab_ready, 2)

            with dve.Fori(0, NG) as b:
                for step in range(PAIRS + 2):
                    if step < PAIRS:
                        p = step
                        dve.wait_ge(ew_s, b * PAIRS + p + 1)
                        w = ew[:, p % EW, :, :]
                        nc.vector.scalar_tensor_tensor(out=w, in0=w, scalar=SLOPE, in1=w, op0=ALU.mult,
                                                       op1=ALU.max).then_inc(ew_z, 1)
                    if 0 <= step - 1 < PAIRS:
                        p = step - 1
                        if p % 2 == 0:
                            dve.wait_ge(adj_loaded[p // 2], b * 16 + 16)
                        dve.wait_ge(ew_x, b * PAIRS + p + 1)
                        w = ew[:, p % EW, :, :]
                        nc.vector.scalar_tensor_tensor(out=w, in0=w, scalar=F32_MAX,
                                                       in1=adj_ring[:, 2 * p:2 * p + 2, :].bitcast(f32),
                                                       op0=ALU.min, op1=ALU.mult).then_inc(ew_m, 1)
                    if 0 <= step - 2 < PAIRS:
                        p = step - 2
                        dve.wait_ge(ehi_ready, b * PAIRS + p + 1)
                        nc.vector.tensor_tensor(e_lo[:, p % ER, :, :], ew[:, p % EW, :, :],
                                                e_hi[:, p % ER, :, :].bitcast(f32), ALU.subtract
                                                ).then_inc(elo_ready, 1)
                    if step == 5:
                        dve.wait_ge(adj_pe, b * 4 + 4)
                        nc.vector.tensor_tensor(gate_z[:, :, :], ps[:, 4:8, D:DX],
                                                gate_x[:, bass.ds(b * GT, GT), :], ALU.add).then_inc(gz_ready, 1)
                        nc.vector.tensor_tensor(yb[:, :, :], ps[:, 4:8, 0:D],
                                                bgc_bc[:, :].unsqueeze(1).broadcast_to([P, GT, D]), ALU.add
                                                ).then_inc(xb_free, 1)
                    if step == 7:
                        dve.wait_ge(gt_ready, b + 1)
                        nc.vector.tensor_scalar(gate[:, :, :], gate_t[:, :, :], 0.5, 0.5, ALU.mult, ALU.add
                                                ).then_inc(gate_ready, 1)
                        dve.wait_ge(gate_ready, b + 1)
                        dve.wait_ge(xb_free, b + 2)
                        for t in range(GT):
                            last = nc.vector.tensor_scalar(yb[:, t, :], yb[:, t, :], gate[:, t, 1:2], None, ALU.mult)
                        last.then_inc(ybs_ready, 1)
                dve.wait_ge(e_used, b * PAIRS + (ER + PAIRS))
                nc.vector.tensor_scalar(e_sum[:, :], ps[:, 0:4, D], EPS_ATT, None, ALU.add).then_inc(esum_ready, 1)
                dve.wait_ge(esum_ready, b + 1)
                nc.vector.reciprocal(e_rsum[:, :], e_sum[:, :]).then_inc(ersum_ready, 1)
                dve.wait_ge(ersum_ready, b + 1)
                nc.vector.tensor_tensor(coef_a[:, :], e_rsum[:, :], gate[:, :, 0], ALU.mult).then_inc(coef_ready, 1)
                dve.wait_ge(coef_ready, b + 1)
                dve.wait_ge(ybs_ready, b + 1)
                for t in range(GT):
                    last = nc.vector.scalar_tensor_tensor(out=yb[:, t, :], in0=ps[:, t, 0:D],
                                                          scalar=coef_a[:, t:t + 1], in1=yb[:, t, :],
                                                          op0=ALU.mult, op1=ALU.add)
                last.then_inc(xa_free, 1)
                dve.wait_ge(yt_ready, b + 1)
                nc.vector.tensor_scalar(y_t[:, :, :], y_t[:, :, :], 0.5, 0.5, ALU.mult, ALU.add).then_inc(yh_ready, 1)
                dve.wait_ge(yh_ready, b + 1)
                nc.vector.tensor_tensor(y_t[:, :, :], x_sb[:, bass.ds(b * GT, GT), :], y_t[:, :, :], ALU.add
                                        ).then_inc(x1_ready, 1)
                dve.wait_ge(x1_ready, b + 1)
                for t in range(GT):
                    nc.vector.bn_stats(stats[:, t, :], y_t[:, t, :]).then_inc(stats_d, 1)
                nc.vector.tensor_copy(x_sb[:, bass.ds(b * GT, GT), :], y_t[:, :, :]).then_inc(x1_kept, 1)
                dve.wait_ge(stats_d, b * GT + (NT + GT))
                dve.wait_ge(mv_ready, b * GT + NT)
                nc.vector.memset(wait_cell[:, :], 0.0)
                for t in range(GT):
                    nc.vector.bn_aggr(mv_block[:, t, :], stats[:, t, :]).then_inc(mvb_ready, 1)
                dve.wait_ge(mvb_ready, b * GT + GT)
                nc.vector.tensor_copy(mean_var[:, bass.ds(b * GT, GT), :], mv_block[:, :, :]).then_inc(mv_ready, GT)

            dve.wait_ge(w1_loaded, 48)
            nc.vector.tensor_copy(w1_hi[:, :, :], w1_raw[:, :, :]).then_inc(w1_hi_s, 1)
            dve.wait_ge(w1_hi_s, 1)
            nc.vector.tensor_tensor(w1_lo[:, :, :], w1_raw[:, :, :], w1_hi[:, :, :].bitcast(f32), ALU.subtract
                                    ).then_inc(w1_s, 1)
            dve.wait_ge(rstd_ready, NG + 1)

            def add_bias(g):
                xs = x_sb[:, g * GT:(g + 1) * GT, :]
                dve.wait_ge(z_ready, NG + g + 1)
                nc.vector.tensor_tensor(xs, xs, bias_bc[:, :].unsqueeze(1).broadcast_to([P, GT, D]), ALU.add
                                        ).then_inc(xbias_ready, 1)

            normalise(NG, rstd)
            normalise(NG + 1, rstd)
            for g in range(NG):
                relu_stage_lo(NG + g)
                for m in range(KD):
                    n = g * KD + m
                    dve.wait_ge(h1_hi, n + 1)
                    nc.vector.tensor_tensor(hh_lo[:, m, g * GN:(g + 1) * GN], ps[:, 2 + m, :],
                                            hh_hi[:, m, g * GN:(g + 1) * GN].bitcast(f32), ALU.subtract
                                            ).then_inc(h1_lo, 1)
                for t in range(GT):
                    j = g * GT + t
                    dve.wait_ge(s1_hi, j + 1)
                    nc.vector.tensor_copy(v_sb[:, j:j + 1], ps[:, 4 + t, D:D + 1])
                    nc.vector.tensor_tensor(s_lo[:, j, :], ps[:, 4 + t, 0:D], s_hi[:, j, :].bitcast(f32),
                                            ALU.subtract).then_inc(s1_lo, 1)
                if g + 2 < NG:
                    normalise(NG + g + 2, rstd)
                add_bias(g)
            dve.wait_ge(s1_lo, NT)
            nc.vector.tensor_reduce(v_max[:, :], v_sb[:, :], AX.X, ALU.max).then_inc(vmax_s, 1)
            dve.wait_ge(vgmax_s, 1)
            nc.vector.tensor_scalar(v_ngmax[:, :], v_gmax[:, :], -1.0, None, ALU.mult).then_inc(vneg_s, 1)

            def masked_half(i, s, h):
                dve.wait_ge(e_done, i * 2 + h + 1)
                dve.wait_ge(mask_ready, i + 1)
                if not (isinstance(i, int) and i == 0 and h == 0):
                    dve.wait_ge(em_ready, i * 2 + h)
                nc.vector.memset(wait_cell[:, :], 0.0)
                nc.vector.tensor_tensor_reduce(
                    out=em[:, s, h * 1024:(h + 1) * 1024], in0=ps[:, 2 * h:2 * h + 2, :],
                    in1=mask[:, s, h * 1024:(h + 1) * 1024].rearrange("p (a b) -> p a b", a=2),
                    scale=1.0, scalar=-3.0e38, op0=ALU.add, op1=ALU.max,
                    accum_out=row_max2[:, s, h:h + 1]).then_inc(em_ready, 1)

            def row_maximum(i, s):
                dve.wait_ge(em_ready, i * 2 + 2)
                nc.vector.tensor_reduce(neg_max[:, s:s + 1], row_max2[:, s, :], AX.X, ALU.max, negate=True
                                        ).then_inc(nmax_ready, 1)

            def transposed_lo(i, s, q):
                dve.wait_ge(pthi_ready, i * 4 + q + 1)
                nc.vector.tensor_tensor(pt_lo[:, s, 4 * q:4 * q + 4, :],
                                        ps[:, 4 + q % 2, :].rearrange("p (t c) -> p t c", t=4),
                                        pt_hi[:, s, 4 * q:4 * q + 4, :].bitcast(f32), ALU.subtract
                                        ).then_inc(ptlo_ready, 1)

            def finish_row(i, s, stored):
                dve.wait_ge(p_ready, i + 1)
                nc.vector.reciprocal(row_rsum[:, s:s + 1], row_sum[:, s:s + 1]).then_inc(rr_ready, 1)
                nc.vector.tensor_scalar(row_flag[:, s:s + 1], neg_max[:, s:s + 1], 0.5 * NEG_BIG,
                                        node_att[:, bass.ds(i, 1)], ALU.is_lt, ALU.mult).then_inc(rf_ready, 1)
                dve.wait_ge(rr_ready, i + 1)
                dve.wait_ge(rf_ready, i + 1)
                nc.vector.tensor_tensor(row_coef[:, s:s + 1], row_rsum[:, s:s + 1], row_flag[:, s:s + 1], ALU.mult
                                        ).then_inc(rc_ready, 1)
                dve.wait_ge(rc_ready, i + 1)
                dve.wait_ge(o_done, i + 1)
                if stored is not None:
                    dve.wait_ge(out_stored[s], stored)
                nc.vector.scalar_tensor_tensor(out=o_sb[:, s, :], in0=ps[:, 6 + s, 0:D],
                                               scalar=row_coef[:, s:s + 1], in1=x_sb[:, bass.ds(i, 1), :].squeeze(1),
                                               op0=ALU.mult, op1=ALU.add).then_inc(o_ready, 1)

            def row_pair_step(i, s, stored):
                masked_half(i + 1, 1 - s, 0)
                transposed_lo(i, s, 0)
                transposed_lo(i, s, 1)
                masked_half(i + 1, 1 - s, 1)
                row_maximum(i + 1, 1 - s)
                transposed_lo(i, s, 2)
                transposed_lo(i, s, 3)
                finish_row(i, s, stored)

            masked_half(0, 0, 0)
            masked_half(0, 0, 1)
            row_maximum(0, 0)
            dve.wait_ge(vgsum_s, 1)
            nc.vector.reciprocal(v_rsum[:, :], v_gsum[:, :]).then_inc(vr_s, 1)
            dve.wait_ge(vr_s, 1)
            nc.vector.tensor_scalar(node_att[:, :], v_exp[:, :], v_rsum[:, 0:1], None, ALU.mult
                                    ).then_inc(natt_ready, 1)
            dve.wait_ge(natt_ready, 1)
            row_pair_step(0, 0, None)
            row_pair_step(1, 1, None)
            with dve.Fori(1, NT // 2 - 1) as i:
                for s in range(2):
                    row_pair_step(i * 2 + s, s, i * 16)
            row_pair_step(NT - 2, 0, 16 * (NT // 2 - 1))
            for q in range(4):
                transposed_lo(NT - 1, 1, q)
            finish_row(NT - 1, 1, 16 * (NT // 2 - 1))

        @block.tensor
        def _(pe):
            def transpose_group(n):
                pe.wait_ge(z_ready, n + 1)
                if n == 0:
                    pe.wait_ge(consts_ready, 1)
                if n >= 1:
                    pe.wait_ge(sthi_ready, n)
                    pe.wait_ge(stlo_ready, n)
                for t in range(GT):
                    for k in range(KD):
                        last = nc.tensor.transpose(ps[:, k, t * P:(t + 1) * P],
                                                   z_sb[:, n % 2, t, k * P:(k + 1) * P], ident[:, :])
                last.then_inc(tr_done, 1)

            def stage(part, n, cols):
                return lambda k: part[:, n % 2, k, cols]

            transpose_group(0)
            for g in range(NG):
                pe.wait_ge(sthi_ready, g + 1)
                pe.wait_ge(stlo_ready, g + 1)
                if g == 0:
                    pe.wait_ge(wsplit, 1)
                if g + 1 < NG:
                    transpose_group(g + 1)
                every = slice(0, GN)
                if g >= 2:
                    pe.wait_ge(sl_ready, g - 1)
                three_products(ps[:, 6 + g % 2, :], lambda k: ul_hi[:, k, :], lambda k: ul_lo[:, k, :],
                               stage(stage_hi, g, every), stage(stage_lo, g, every)).then_inc(sl_done, 1)
                for t in range(GT):
                    j = g * GT + t
                    cols = slice(t * P, (t + 1) * P)
                    hi, lo = stage(stage_hi, g, cols), stage(stage_lo, g, cols)
                    if j >= 3:
                        pe.wait_ge(g_lo, j - 2)
                    three_products(ps[:, 2 + j % 3, :], hi, lo, lambda k: w0_hi[:, k, :], lambda k: w0_lo[:, k, :]
                                   ).then_inc(g_done, 1)
                    last = three_products(ps[:, 5, j * 6:(j + 1) * 6], hi, lo, lambda k: xc_hi[:, k, :],
                                          lambda k: xc_lo[:, k, :])
                last.then_inc(stage_used, 1)

            pe.wait_ge(ab_ready, 1)
            pe.wait_ge(sl_ready, NG)
            pe.wait_ge(g_lo, NT)
            with pe.Fori(0, NG) as b:
                pe.wait_ge(xb_free, b + 1)
                for j in range(NT):
                    if j % 4 == 0:
                        pe.wait_ge(adj_loaded[j // 4], b * 16 + 16)
                    for t in range(GT):
                        lhs = adj_ring[:, j, t * P:(t + 1) * P]
                        nc.tensor.matmul(ps[:, 4 + t, 0:DX], lhs, ab_hi[:, j, 1, :], start=(j == 0), stop=False)
                        last = nc.tensor.matmul(ps[:, 4 + t, 0:DX], lhs, ab_lo[:, j, 1, :], start=False,
                                                stop=(j == NT - 1))
                    if j % 4 == 3:
                        last.then_inc(adj_pe, 1)
                pe.wait_ge(xa_free, b + 1)
                for p in range(PAIRS):
                    pe.wait_ge(elo_ready, b * PAIRS + (EW + p + 1))
                    for h in range(2):
                        j = 2 * p + h
                        for t in range(GT):
                            cols = slice(t * P, (t + 1) * P)
                            hi, lo = e_hi[:, p % ER, h, cols], e_lo[:, p % ER, h, cols]
                            nc.tensor.matmul(ps[:, t, 0:DX], hi, ab_hi[:, j, 0, :], start=(j == 0), stop=False)
                            nc.tensor.matmul(ps[:, t, 0:D], hi, ab_lo[:, j, 0, 0:D], start=False, stop=False)
                            last = nc.tensor.matmul(ps[:, t, 0:DX], lo, ab_hi[:, j, 0, :], start=False,
                                                    stop=(j == NT - 1))
                    last.then_inc(e_used, 1)

            transpose_group(NG)
            pe.wait_ge(w1_s, 1)
            for g in range(NG):
                n = NG + g
                pe.wait_ge(sthi_ready, n + 1)
                pe.wait_ge(stlo_ready, n + 1)
                if g + 1 < NG:
                    transpose_group(n + 1)
                every = slice(0, GN)
                for m in range(KD):
                    if g >= 1:
                        pe.wait_ge(h1_lo, (g - 1) * KD + m + 1)
                    rows = slice(m * P, (m + 1) * P)
                    three_products(ps[:, 2 + m, :], lambda k: w1_hi[:, k, rows], lambda k: w1_lo[:, k, rows],
                                   stage(stage_hi, n, every), stage(stage_lo, n, every)).then_inc(h1_done, 1)
                for t in range(GT):
                    if g >= 1:
                        pe.wait_ge(s1_lo, (g - 1) * GT + t + 1)
                    cols = slice(t * P, (t + 1) * P)
                    wide = slice(D, 2 * D + 2)
                    last = three_products(ps[:, 4 + t, 0:DX], stage(stage_hi, n, cols), stage(stage_lo, n, cols),
                                          lambda k: w1_hi[:, k, wide], lambda k: w1_lo[:, k, wide])
                    last.then_inc(s1_done, 1)

            def score_half(i, s, h, first):
                if not first:
                    pe.wait_ge(em_ready, i * 2 + (h - 1))
                for c in range(2 * h, 2 * h + 2):
                    cols = slice(c * GN, (c + 1) * GN)
                    last = three_products(ps[:, c, :], lambda k: hs_hi[:, s, k, :], lambda k: hs_lo[:, s, k, :],
                                          lambda k: hh_hi[:, k, cols], lambda k: hh_lo[:, k, cols])
                last.then_inc(e_done, 1)

            def transpose_quarter(i, s, q, first):
                if q >= 2 or not first:
                    pe.wait_ge(ptlo_ready, i * 4 + (q - 1))
                for t in range(4):
                    last = nc.tensor.transpose(ps[:, 4 + q % 2, t * P:(t + 1) * P],
                                               em[:, s, (4 * q + t) * P:(4 * q + t + 1) * P], ident[:, :])
                last.then_inc(t_done, 1)

            def row_products(i, s, first):
                if not first:
                    pe.wait_ge(o_ready, i - 1)
                for q in range(4):
                    pe.wait_ge(ptlo_ready, i * 4 + q + 1)
                    for j in range(4 * q, 4 * q + 4):
                        nc.tensor.matmul(ps[:, 6 + s, 0:D], pt_hi[:, s, j, :], s_hi[:, j, :], start=(j == 0),
                                         stop=False)
                        nc.tensor.matmul(ps[:, 6 + s, 0:D], pt_hi[:, s, j, :], s_lo[:, j, :], start=False,
                                         stop=False)
                        last = nc.tensor.matmul(ps[:, 6 + s, 0:D], pt_lo[:, s, j, :], s_hi[:, j, :], start=False,
                                                stop=(j == NT - 1))
                last.then_inc(o_done, 1)

            def row_step(i, s, first, first_o):
                pe.wait_ge(hs_ready, i + 2)
                score_half(i + 1, 1 - s, 0, False)
                pe.wait_ge(p_ready, i + 1)
                transpose_quarter(i, s, 0, first)
                transpose_quarter(i, s, 1, first)
                score_half(i + 1, 1 - s, 1, False)
                transpose_quarter(i, s, 2, first)
                transpose_quarter(i, s, 3, first)
                row_products(i, s, first_o)

            pe.wait_ge(hs_ready, 1)
            pe.wait_ge(s1_lo, NT)
            score_half(0, 0, 0, True)
            score_half(0, 0, 1, True)
            row_step(0, 0, True, True)
            row_step(1, 1, False, True)
            with pe.Fori(1, NT // 2 - 1) as i:
                for s in range(2):
                    row_step(i * 2 + s, s, False, False)
            row_step(NT - 2, 0, False, False)
            pe.wait_ge(p_ready, NT)
            for q in range(4):
                transpose_quarter(NT - 1, 1, q, False)
            row_products(NT - 1, 1, False)


_INS = ["x", "adj", "adj_t", "L0_gnn_W_sa", "L0_gnn_a_sa", "L0_gnn_W_gcnb", "L0_gnn_b_gcnb", "L0_gnn_Wa", "L0_gnn_ba",
        "L0_gnn_Wb", "L0_gnn_bb", "L1_gnn_weight", "L1_gnn_bias", "L1_gnn_node_w", "L1_gnn_edge_w"]


def kernel(**inputs):
    import numpy as _np
    import concourse.bacc as _bacc
    from concourse import mybir as _mybir
    from concourse.bass_utils import run_bass_kernel_spmd as _run

    nc = _bacc.Bacc("TRN2", target_bir_lowering=False, num_devices=1)
    arrays, args = {}, []
    for name in _INS:
        a = _np.asarray(inputs["adj"]).T if name == "adj_t" else inputs[name]
        a = _np.ascontiguousarray(a)
        arrays[f"in_{name}_dram"] = a
        args.append(nc.dram_tensor(f"in_{name}_dram", a.shape, _mybir.dt.from_np(a.dtype), kind="ExternalInput").ap())
    x = arrays["in_x_dram"]
    args.append(nc.dram_tensor("out_0_dram", x.shape, _mybir.dt.from_np(x.dtype), kind="ExternalOutput").ap())
    build_two_graph_blocks(nc, *args)
    r = _run(nc, [arrays], core_ids=[0])
    return r.results[0]["out_0_dram"]
```

```python
import concourse.bass as bass
from concourse import mybir
from contextlib import ExitStack


def build_two_graph_blocks(nc: bass.Bass, x, adj, adj_t, W_sa, a_sa, W_gcnb, b_gcnb, Wa, ba, Wb, bb,
                           weight, bias, node_w, edge_w, out):
    f32, f32r = mybir.dt.float32, mybir.dt.float32r
    ALU = mybir.AluOpType
    ACT = mybir.ActivationFunctionType
    AX = mybir.AxisListType
    RED = bass.bass_isa.ReduceOp

    P = 128
    N, D = x.shape
    KD = D // P
    NT = N // P
    GT = 4
    GN = GT * P
    NG = N // GN
    PAIRS = NT // 2
    EW = 4
    ER = 4
    ZR = 3
    DX = D + 2
    SLOPE = 0.01
    NEG_BIG = 9.0e15
    F32_MAX = 3.0e38
    EPS_LN, EPS_ATT = 1e-5, 1e-5

    ctx = ExitStack()
    with ctx:
        def sb(name, shape, dt=f32, on=ctx):
            return on.enter_context(nc.sbuf_tensor(name, shape, dt))

        def sem(name):
            return ctx.enter_context(nc.semaphore(name))

        x_sb = sb("x_sb", [P, NT, D])
        z_sb = sb("z_sb", [P, ZR, GT, D])
        stage_hi = sb("stage_hi", [P, 2, KD, GN], f32r)
        stage_lo = sb("stage_lo", [P, 2, KD, GN], f32r)
        ident = sb("ident", [P, P])
        stats = sb("stats", [P, NT, 6])
        mean_var = sb("mean_var", [P, NT, 2])
        rstd = sb("rstd", [P, NT])
        minus_half = sb("minus_half", [P, NT])
        w1_raw = sb("w1_raw", [P, KD, 2 * D + 2])
        bgc_bc = sb("bgc_bc", [P, D])
        bias_bc = sb("bias_bc", [P, D])
        gate_bias = sb("gate_bias", [P, 2])
        wait_cell = sb("wait_cell", [P, 1])

        l0 = ExitStack()
        with l0:
            ab_hi = sb("ab_hi", [P, NT, 2, DX], f32r, l0)
            ab_lo = sb("ab_lo", [P, NT, 2, DX], f32r, l0)
            adj_ring = sb("adj_ring", [P, NT, GN], f32r, l0)
            e_hi = sb("e_hi", [P, ER, 2, GN], f32r, l0)
            e_lo = sb("e_lo", [P, ER, 2, GN], f32r, l0)
            sl_bc = sb("sl_bc", [P, N], f32, l0)
            extras = sb("extras", [P, NT, 6], f32, l0)
            gate_x = sb("gate_x", [P, NT, 2], f32, l0)
            gate_z = sb("gate_z", [P, GT, 2], f32, l0)
            gate_t = sb("gate_t", [P, GT, 2], f32, l0)
            gate = sb("gate", [P, GT, 2], f32, l0)
            mv_block = sb("mv_block", [P, GT, 2], f32, l0)
            e_sum = sb("e_sum", [P, GT], f32, l0)
            e_rsum = sb("e_rsum", [P, GT], f32, l0)
            coef_a = sb("coef_a", [P, GT], f32, l0)
            yb, y_t = z_sb[:, 0, :, :], z_sb[:, 2, :, :]
            w0 = ExitStack()
            with w0:
                w0_raw = sb("w0_raw", [P, KD, 2 * D], f32, w0)
                a_bc = sb("a_bc", [P, 2 * D], f32, w0)
                w0_hi = sb("w0_hi", [P, KD, 2 * D], f32r, w0)
                w0_lo = sb("w0_lo", [P, KD, 2 * D], f32r, w0)
                xc_raw = sb("xc_raw", [P, KD, 6], f32, w0)
                xc_hi = sb("xc_hi", [P, KD, 6], f32r, w0)
                xc_lo = sb("xc_lo", [P, KD, 6], f32r, w0)
                u_left = sb("u_left", [P, KD], f32, w0)
                ul_hi = sb("ul_hi", [P, KD, P], f32r, w0)
                ul_lo = sb("ul_lo", [P, KD, P], f32r, w0)
                u_junk = z_sb[:, 2, :, :]
            ew = sb("ew", [P, EW, 2, GN], f32, l0)

        hh_hi = sb("hh_hi", [P, KD, N], f32r)
        hh_lo = sb("hh_lo", [P, KD, N], f32r)
        s_hl = sb("s_hl", [P, NT, 2, D], f32r)
        w1_hi = sb("w1_hi", [P, KD, 2 * D + 2], f32r)
        w1_lo = sb("w1_lo", [P, KD, 2 * D + 2], f32r)
        mask = sb("mask", [P, 2, N])
        em = sb("em", [P, 2, N])
        pt_hi = sb("pt_hi", [P, 2, NT, P], f32r)
        pt_lo = sb("pt_lo", [P, 2, NT, P], f32r)
        hs_hi = sb("hs_hi", [P, 2, KD, P], f32r)
        hs_lo = sb("hs_lo", [P, 2, KD, P], f32r)
        row_max2 = sb("row_max2", [P, 2, 2])
        neg_max = sb("neg_max", [P, 2])
        row_sum = sb("row_sum", [P, 2])
        row_rsum = sb("row_rsum", [P, 2])
        row_flag = sb("row_flag", [P, 2])
        row_coef = sb("row_coef", [P, 2])
        o_part = sb("o_part", [P, 2, D])
        o_sb = sb("o_sb", [P, 2, D])
        v_sb = sb("v_sb", [P, NT])
        v_max = sb("v_max", [P, 1])
        v_gmax = sb("v_gmax", [P, 1])
        v_ngmax = sb("v_ngmax", [P, 1])
        v_exp = sb("v_exp", [P, NT])
        v_sum = sb("v_sum", [P, 1])
        v_gsum = sb("v_gsum", [P, 1])
        v_rsum = sb("v_rsum", [P, 1])
        node_att = sb("node_att", [P, NT])

        ps = ctx.enter_context(nc.psum_tensor("ps", [P, 8, GN], f32))

        x_loaded = [sem(f"x_loaded{g}") for g in range(NG)]
        cols_loaded = sem("cols_loaded")
        w0_loaded, w1_loaded, vec_loaded = sem("w0_loaded"), sem("w1_loaded"), sem("vec_loaded")
        consts_ready = sem("consts_ready")
        ident_z = sem("ident_z")
        stats_d = sem("stats_d")
        mv_ready = sem("mv_ready")
        ve_ready = sem("ve_ready")
        rstd_ready = sem("rstd_ready")
        u_ready, wsplit_hi, wsplit = sem("u_ready"), sem("wsplit_hi"), sem("wsplit")
        z_ready = sem("z_ready")
        tr_done = sem("tr_done")
        sthi_ready, stlo_ready = sem("sthi_ready"), sem("stlo_ready")
        stage_used = sem("stage_used")
        g_done, g_hi, g_lo = sem("g_done"), sem("g_hi"), sem("g_lo")
        sl_done, sl_ready = sem("sl_done"), sem("sl_ready")
        exs_ready, ab_ready = sem("exs_ready"), sem("ab_ready")
        abx_hi = sem("abx_hi")
        adj_loaded = [sem(f"adj_loaded{g}") for g in range(4)]
        adj_pe = sem("adj_pe")
        ew_s, ew_z, ew_x, ew_m = sem("ew_s"), sem("ew_z"), sem("ew_x"), sem("ew_m")
        ehi_ready = sem("ehi_ready")
        elo_ready = sem("elo_ready")
        e_used = sem("e_used")
        xb_free, xa_free = sem("xb_free"), sem("xa_free")
        gz_ready, gt_ready, gate_ready = sem("gz_ready"), sem("gt_ready"), sem("gate_ready")
        yb_ready, esum_ready, ersum_ready, coef_ready = (sem("yb_ready"), sem("esum_ready"),
                                                         sem("ersum_ready"), sem("coef_ready"))
        ybs_ready, yt_ready, yh_ready, x1_ready = sem("ybs_ready"), sem("yt_ready"), sem("yh_ready"), sem("x1_ready")
        x1_kept, mvb_ready = sem("x1_kept"), sem("mvb_ready")
        w1_hi_s, w1_s = sem("w1_hi_s"), sem("w1_s")
        xbias_ready = sem("xbias_ready")
        h1_done, h1_hi, h1_lo = sem("h1_done"), sem("h1_hi"), sem("h1_lo")
        s1_done, s1_hi, s1_lo, v_ready = sem("s1_done"), sem("s1_hi"), sem("s1_lo"), sem("v_ready")
        vmax_s, vgmax_s, vneg_s, vexp_s, vgsum_s, vr_s, natt_ready = (
            sem("vmax_s"), sem("vgmax_s"), sem("vneg_s"), sem("vexp_s"), sem("vgsum_s"), sem("vr_s"),
            sem("natt_ready"))
        mask_loaded = [sem("mask_loaded0"), sem("mask_loaded1")]
        mask_ready = sem("mask_ready")
        hs_ready = sem("hs_ready")
        e_done = sem("e_done")
        em_ready = sem("em_ready")
        nmax_ready, p_ready = sem("nmax_ready"), sem("p_ready")
        t_done = sem("t_done")
        pthi_ready, ptlo_ready = sem("pthi_ready"), sem("ptlo_ready")
        o_done, op_ready, o_ready = sem("o_done"), sem("op_ready"), sem("o_ready")
        rr_ready, rf_ready, rc_ready = sem("rr_ready"), sem("rf_ready"), sem("rc_ready")
        out_stored = [sem("out_stored0"), sem("out_stored1")]

        xg = x.rearrange("(g t p) d -> g p t d", t=GT, p=P)
        adjt_v = adj_t.rearrange("(q t p) n -> q p t n", q=4, p=P)
        adj_v = adj.rearrange("(t p) n -> t p n", p=P)
        out_v = out.rearrange("(t p) d -> t p d", p=P)

        def kview(w):
            return w.rearrange("(k p) c -> p k c", p=P)

        def three_products(pe_out, lhs_hi, lhs_lo, rhs_hi, rhs_lo):
            terms = [(lhs_hi, rhs_hi), (lhs_hi, rhs_lo), (lhs_lo, rhs_hi)]
            for n, (a, b) in enumerate(terms):
                for k in range(KD):
                    last = nc.tensor.matmul(pe_out, a(k), b(k), start=(n == 0 and k == 0),
                                            stop=(n == 2 and k == KD - 1))
            return last

        block = ctx.enter_context(nc.Block())

        @block.sync
        def _(sp):
            for g in range(NG):
                sp.dma_start(x_sb[:, g * GT:(g + 1) * GT, :], xg[g]).then_inc(x_loaded[g], 16)
                if g == 0:
                    sp.dma_start(w0_raw[:, :, 0:D], kview(W_sa)).then_inc(w0_loaded, 16)
                    sp.dma_start(w0_raw[:, :, D:2 * D], kview(W_gcnb)).then_inc(w0_loaded, 16)
                    sp.dma_start(a_bc[:, :], a_sa[0].partition_broadcast(P)).then_inc(w0_loaded, 16)
            sp.dma_start(bgc_bc[:, :], b_gcnb.partition_broadcast(P)).then_inc(vec_loaded, 16)
            sp.dma_start(bias_bc[:, :], bias.partition_broadcast(P)).then_inc(vec_loaded, 16)
            sp.dma_start(gate_bias[:, 0:1], ba.partition_broadcast(P)).then_inc(vec_loaded, 16)
            sp.dma_start(gate_bias[:, 1:2], bb.partition_broadcast(P)).then_inc(vec_loaded, 16)
            sp.dma_start(w1_raw[:, :, 0:D], kview(edge_w)).then_inc(w1_loaded, 16)
            sp.dma_start(w1_raw[:, :, D:2 * D], kview(weight)).then_inc(w1_loaded, 16)
            sp.dma_start(w1_raw[:, :, 2 * D:2 * D + 1], kview(node_w),
                         allow_slow_non_contiguous=True).then_inc(w1_loaded, 16)

            sp.wait_ge(e_used, ER + NG * PAIRS)
            sp.wait_ge(x1_kept, NG)
            for t in range(2):
                sp.dma_start(mask[:, t, :], adj_v[t]).then_inc(mask_loaded[t], 16)
            with sp.Fori(0, NT // 2 - 1) as i:
                for s in range(2):
                    sp.wait_ge(em_ready, i * 4 + 2 * s + 2)
                    sp.dma_start(mask[:, s, :], adj_v[i * 2 + s + 2]).then_inc(mask_loaded[s], 16)
                for s in range(2):
                    sp.wait_ge(o_ready, i * 2 + s + 1)
                    sp.dma_start(out_v[i * 2 + s], o_sb[:, s, :]).then_inc(out_stored[s], 16)
            for s in range(2):
                sp.wait_ge(o_ready, NT - 1 + s)
                sp.dma_start(out_v[NT - 2 + s], o_sb[:, s, :]).then_inc(out_stored[s], 16)
            for s in range(2):
                sp.wait_ge(out_stored[s], 16 * (NT // 2))

        @block.gpsimd
        def _(pool):
            def load_adj_quarter(b, q):
                pool.dma_start(adj_ring[:, q * 4:(q + 1) * 4, :],
                               adjt_v[q][:, :, bass.ds(b * GN, GN)]).then_inc(adj_loaded[q], 16)

            nc.gpsimd.memset(ident[:, :], 0.0).then_inc(ident_z, 1)
            nc.gpsimd.memset(minus_half[:, :], -0.5)
            nc.gpsimd.memset(xc_raw[:, :, 5:6], 0.0)
            nc.gpsimd.memset(w1_raw[:, :, 2 * D + 1:2 * D + 2], 0.0)
            pool.wait_ge(ident_z, 1)
            nc.gpsimd.affine_select(out=ident[:, :], in_=ident[:, :], compare_op=ALU.not_equal, fill=1.0, base=0,
                                    pattern=[[-1, P]], channel_multiplier=1).then_inc(consts_ready, 1)
            def group_rstd(n):
                g = n % NG
                sl = slice(g * GT, (g + 1) * GT)
                pool.wait_ge(mv_ready, GT * (n + 1))
                if n >= NG:
                    pool.wait_ge(z_ready, g + 1)
                nc.gpsimd.tensor_scalar(rstd[:, sl], mean_var[:, sl, 1], EPS_LN, None, ALU.add).then_inc(ve_ready, 1)
                pool.wait_ge(ve_ready, n + 1)
                nc.gpsimd.tensor_tensor(rstd[:, sl], rstd[:, sl], minus_half[:, sl], ALU.pow
                                        ).then_inc(rstd_ready, 1)

            for g in range(NG):
                group_rstd(g)
                load_adj_quarter(0, g)
            with pool.Fori(1, NG) as b:
                for q in range(4):
                    pool.wait_ge(adj_pe, b * 4 + (q + 1 - 4))
                    pool.wait_ge(ew_m, b * PAIRS + (2 * q + 2 - PAIRS))
                    load_adj_quarter(b, q)
            for g in range(NG):
                group_rstd(NG + g)
            pool.wait_ge(vmax_s, 1)
            nc.gpsimd.partition_all_reduce(v_gmax[:, :], v_max[:, :], P, RED.max).then_inc(vgmax_s, 1)
            def stage_row(i, s):
                nc.gpsimd.tensor_copy(hs_hi[:, s, :, :], hh_hi[:, :, bass.ds(i * P, P)].bitcast(f32))
                nc.gpsimd.tensor_copy(hs_lo[:, s, :, :], hh_lo[:, :, bass.ds(i * P, P)].bitcast(f32)
                                      ).then_inc(hs_ready, 1)
            pool.wait_ge(h1_hi, 2 * NG)
            pool.wait_ge(h1_lo, 2 * NG)
            stage_row(0, 0)
            stage_row(1, 1)
            pool.wait_ge(vexp_s, 1)
            nc.gpsimd.partition_all_reduce(v_gsum[:, :], v_sum[:, :], P, RED.add).then_inc(vgsum_s, 1)
            with pool.Fori(1, NT // 2) as i:
                for s in range(2):
                    pool.wait_ge(e_done, i * 4 + (2 * s + 2 - 4))
                    stage_row(i * 2 + s, s)

        @block.scalar
        def _(act):
            def relu_stage(n):
                act.wait_ge(tr_done, n + 1)
                if 2 <= n < NG + 2:
                    act.wait_ge(stage_used, min(n - 1, NG))
                if n >= NG + 2:
                    act.wait_ge(s1_done, GT * (n - NG - 1))
                tb = 0 if n < NG else 4
                nc.scalar.activation(stage_hi[:, n % 2, :, :], ps[:, tb:tb + 2, :], ACT.Relu).then_inc(sthi_ready, 1)

            for side in range(2):
                for c, w in ((1, Wa), (2, Wb)):
                    act.dma_start(xc_raw[:, :, c + 2 * side:c + 2 * side + 1],
                                  w[0:1, side * D:(side + 1) * D].rearrange("o (k p) -> p k o", p=P),
                                  allow_slow_non_contiguous=True).then_inc(cols_loaded, 16)

            relu_stage(0)
            for g in range(NG):
                if g + 1 < NG:
                    relu_stage(g + 1)
                act.wait_ge(sl_done, g + 1)
                nc.scalar.copy(sl_bc[:, g * GN:(g + 1) * GN], ps[:, 6 + g % 2, :]).then_inc(sl_ready, 1)
                for t in range(GT):
                    j = g * GT + t
                    act.wait_ge(g_done, j + 1)
                    nc.scalar.copy(ab_hi[:, j, :, 0:D], ps[:, 2 + j % 3, :].rearrange("p (c d) -> p c d", c=2)
                                   ).then_inc(g_hi, 1)

            def score_sum(b, p):
                if p >= PAIRS:
                    b, p = b + 1, p - PAIRS
                for h in range(2):
                    last = nc.scalar.activation(ew[:, p % EW, h, :], sl_bc[:, bass.ds(b * GN, GN)], ACT.Identity,
                                                bias=extras[:, 2 * p + h, 0:1])
                last.then_inc(ew_s, 1)

            def score_exp(b, p):
                act.wait_ge(ew_z, b * PAIRS + p + 1)
                w = ew[:, p % EW, :, :]
                nc.scalar.activation(w, w, ACT.Exp, scale=-1.0).then_inc(ew_x, 1)

            def score_hi(b, p):
                act.wait_ge(ew_m, b * PAIRS + p + 1)
                act.wait_ge(e_used, b * PAIRS + p + 1)
                nc.scalar.copy(e_hi[:, p % ER, :, :], ew[:, p % EW, :, :]).then_inc(ehi_ready, 1)

            def score_block(b, first, last):
                for p in range(PAIRS):
                    if not last or p + 2 < PAIRS:
                        if not first or p + 2 >= EW:
                            act.wait_ge(elo_ready, b * PAIRS + p + 3)
                        score_exp(b, p + 1)
                        score_sum(b, p + 2)
                    elif p + 1 < PAIRS:
                        score_exp(b, p + 1)
                    score_hi(b, p)
                    if p == 5:
                        act.wait_ge(gz_ready, b + 1)
                        nc.scalar.activation(gate_t[:, :, :], gate_z[:, :, :], ACT.Tanh, scale=0.5
                                             ).then_inc(gt_ready, 1)
                    if p == 3 and not first:
                        y_tanh(b - 1)

            def y_tanh(b):
                act.wait_ge(xa_free, b + 2)
                nc.scalar.activation(y_t, y_t, ACT.Tanh, scale=0.5).then_inc(yt_ready, 1)

            act.wait_ge(exs_ready, 1)
            act.wait_ge(sl_ready, NG)
            score_sum(0, 0)
            score_sum(0, 1)
            score_exp(0, 0)
            score_block(0, True, False)
            with act.Fori(1, NG - 1) as b:
                score_block(b, False, False)
            score_block(NG - 1, False, True)
            relu_stage(NG)
            y_tanh(NG - 1)

            for g in range(NG):
                for m in range(KD):
                    n = g * KD + m
                    act.wait_ge(h1_done, n + 1)
                    nc.scalar.copy(hh_hi[:, m, g * GN:(g + 1) * GN], ps[:, 6 + m, :]).then_inc(h1_hi, 1)
                if g + 1 < NG:
                    relu_stage(NG + g + 1)
                for t in range(GT):
                    j = g * GT + t
                    act.wait_ge(s1_done, j + 1)
                    nc.scalar.copy(s_hl[:, j, 0, :], ps[:, t, 0:D]).then_inc(s1_hi, 1)

            def make_mask(s, n):
                act.wait_ge(mask_loaded[s], n)
                nc.scalar.activation(mask[:, s, :], mask[:, s, :], ACT.Copy, bias=-NEG_BIG, scale=NEG_BIG
                                     ).then_inc(mask_ready, 1)

            def exp_row(i, s):
                act.wait_ge(nmax_ready, i + 1)
                nc.scalar.activation(em[:, s, :], em[:, s, :], ACT.Exp, bias=neg_max[:, s:s + 1],
                                     accum_out=row_sum[:, s:s + 1]).then_inc(p_ready, 1)

            def transposed_hi(i, s, q):
                act.wait_ge(t_done, i * 4 + q + 1)
                nc.scalar.copy(pt_hi[:, s, 4 * q:4 * q + 4, :],
                               ps[:, 4 + q % 2, :].rearrange("p (t c) -> p t c", t=4)).then_inc(pthi_ready, 1)

            make_mask(0, 16)
            make_mask(1, 16)
            act.wait_ge(vneg_s, 1)
            nc.scalar.activation(v_exp[:, :], v_sb[:, :], ACT.Exp, bias=v_ngmax[:, 0:1],
                                 accum_out=v_sum[:, :]).then_inc(vexp_s, 1)
            exp_row(0, 0)
            with act.Fori(0, NT // 2 - 1) as i:
                for s in range(2):
                    for q in range(4):
                        transposed_hi(i * 2 + s, s, q)
                    make_mask(s, i * 16 + 32)
                    exp_row(i * 2 + s + 1, 1 - s)
            for s in range(2):
                for q in range(4):
                    transposed_hi(NT - 2 + s, s, q)
                if s == 0:
                    exp_row(NT - 1, 1)

        @block.vector
        def _(dve):
            dve.sem_inc(elo_ready, EW)
            dve.sem_inc(e_used, ER)
            dve.sem_inc(xb_free, 1)
            dve.sem_inc(xa_free, 1)
            nc.vector.memset(ab_hi[:, :, 0, D:D + 1].bitcast(f32), 1.0)
            nc.vector.memset(ab_hi[:, :, 0, D + 1:D + 2].bitcast(f32), 0.0)

            def group_stats(g):
                dve.wait_ge(x_loaded[g], 16)
                for j in range(g * GT, (g + 1) * GT):
                    nc.vector.bn_stats(stats[:, j, :], x_sb[:, j, :]).then_inc(stats_d, 1)
                for j in range(g * GT, (g + 1) * GT):
                    dve.wait_ge(stats_d, j + 1)
                    nc.vector.bn_aggr(mean_var[:, j, :], stats[:, j, :]).then_inc(mv_ready, 1)

            def normalise(n):
                g = n % NG
                dve.wait_ge(rstd_ready, n + 1)
                if n >= ZR:
                    dve.wait_ge(tr_done, n - ZR + 1)
                for t in range(GT):
                    j = g * GT + t
                    last = nc.vector.tensor_scalar(z_sb[:, n % ZR, t, :], x_sb[:, j, :], mean_var[:, j, 0:1],
                                                   rstd[:, j:j + 1], ALU.subtract, ALU.mult)
                last.then_inc(z_ready, 1)

            def relu_stage_lo(n):
                dve.wait_ge(sthi_ready, n + 1)
                tb = 0 if n < NG else 4
                nc.vector.scalar_tensor_tensor(out=stage_lo[:, n % 2, :, :], in0=ps[:, tb:tb + 2, :], scalar=0.0,
                                               in1=stage_hi[:, n % 2, :, :].bitcast(f32), op0=ALU.max,
                                               op1=ALU.subtract).then_inc(stlo_ready, 1)

            def split_weights():
                dve.wait_ge(w0_loaded, 3 * 16)
                for k in range(KD):
                    for side, dst in enumerate((u_left[:, k:k + 1], xc_raw[:, k, 0:1])):
                        nc.vector.tensor_tensor_reduce(out=u_junk[:, 2 * k + side, :], in0=w0_raw[:, k, 0:D],
                                                       in1=a_bc[:, side * D:(side + 1) * D], scale=1.0, scalar=0.0,
                                                       op0=ALU.mult, op1=ALU.add, accum_out=dst).then_inc(u_ready, 1)
                nc.vector.tensor_copy(w0_hi[:, :, :], w0_raw[:, :, :])
                dve.wait_ge(consts_ready, 1)
                dve.wait_ge(cols_loaded, 4 * 16)
                dve.wait_ge(u_ready, 2 * KD)
                ul_b = u_left[:, :].unsqueeze(2).broadcast_to([P, KD, P])
                nc.vector.tensor_copy(xc_hi[:, :, :], xc_raw[:, :, :])
                nc.vector.tensor_copy(ul_hi[:, :, :], ul_b).then_inc(wsplit_hi, 1)
                dve.wait_ge(wsplit_hi, 1)
                nc.vector.tensor_tensor(ul_lo[:, :, :], ul_b, ul_hi[:, :, :].bitcast(f32), ALU.subtract)
                nc.vector.tensor_tensor(xc_lo[:, :, :], xc_raw[:, :, :], xc_hi[:, :, :].bitcast(f32), ALU.subtract)
                nc.vector.tensor_tensor(w0_lo[:, :, :], w0_raw[:, :, :], w0_hi[:, :, :].bitcast(f32), ALU.subtract
                                        ).then_inc(wsplit, 1)

            group_stats(0)
            split_weights()
            normalise(0)
            group_stats(1)
            relu_stage_lo(0)
            normalise(1)
            for g in range(NG):
                if g + 2 < NG:
                    group_stats(g + 2)
                if g + 1 < NG:
                    relu_stage_lo(g + 1)
                if g + 2 < NG:
                    normalise(g + 2)
                for t in range(GT):
                    j = g * GT + t
                    dve.wait_ge(g_hi, j + 1)
                    nc.vector.tensor_tensor(ab_lo[:, j, :, 0:D],
                                            ps[:, 2 + j % 3, :].rearrange("p (c d) -> p c d", c=2),
                                            ab_hi[:, j, :, 0:D].bitcast(f32), ALU.subtract).then_inc(g_lo, 1)

            dve.wait_ge(stage_used, NG)
            nc.vector.tensor_copy(extras[:, :, :], ps[:, 5, 0:NT * 6].rearrange("p (t c) -> p t c", c=6)
                                  ).then_inc(exs_ready, 1)
            dve.wait_ge(exs_ready, 1)
            nc.vector.tensor_copy(ab_hi[:, :, 1, D:DX], extras[:, :, 1:3]).then_inc(abx_hi, 1)
            dve.wait_ge(abx_hi, 1)
            nc.vector.tensor_tensor(ab_lo[:, :, 1, D:DX], extras[:, :, 1:3], ab_hi[:, :, 1, D:DX].bitcast(f32),
                                    ALU.subtract).then_inc(ab_ready, 1)
            dve.wait_ge(vec_loaded, 64)
            nc.vector.tensor_tensor(gate_x[:, :, :], extras[:, :, 3:5],
                                    gate_bias[:, :].unsqueeze(1).broadcast_to([P, NT, 2]), ALU.add
                                    ).then_inc(ab_ready, 1)
            dve.wait_ge(ab_ready, 2)

            def leaky_relu(b, p):
                if p >= PAIRS:
                    b, p = b + 1, p - PAIRS
                dve.wait_ge(ew_s, b * PAIRS + p + 1)
                w = ew[:, p % EW, :, :]
                nc.vector.scalar_tensor_tensor(out=w, in0=w, scalar=SLOPE, in1=w, op0=ALU.mult, op1=ALU.max
                                               ).then_inc(ew_z, 1)

            def mask_pair(b, p):
                if p >= PAIRS:
                    b, p = b + 1, p - PAIRS
                if p % 2 == 0:
                    dve.wait_ge(adj_loaded[p // 2], b * 16 + 16)
                dve.wait_ge(ew_x, b * PAIRS + p + 1)
                w = ew[:, p % EW, :, :]
                nc.vector.scalar_tensor_tensor(out=w, in0=w, scalar=F32_MAX,
                                               in1=adj_ring[:, 2 * p:2 * p + 2, :].bitcast(f32), op0=ALU.min,
                                               op1=ALU.mult).then_inc(ew_m, 1)

            def score_lo(b, p):
                dve.wait_ge(ehi_ready, b * PAIRS + p + 1)
                nc.vector.tensor_tensor(e_lo[:, p % ER, :, :], ew[:, p % EW, :, :],
                                        e_hi[:, p % ER, :, :].bitcast(f32), ALU.subtract).then_inc(elo_ready, 1)

            def read_gcn(b):
                dve.wait_ge(adj_pe, b * 4 + 4)
                nc.vector.tensor_tensor(gate_z[:, :, :], ps[:, 4:8, D:DX], gate_x[:, bass.ds(b * GT, GT), :], ALU.add
                                        ).then_inc(gz_ready, 1)
                nc.vector.tensor_tensor(yb, ps[:, 4:8, 0:D], bgc_bc[:, :].unsqueeze(1).broadcast_to([P, GT, D]),
                                        ALU.add).then_inc(xb_free, 1)

            def apply_gate(b):
                dve.wait_ge(gt_ready, b + 1)
                nc.vector.tensor_scalar(gate[:, :, :], gate_t[:, :, :], 0.5, 0.5, ALU.mult, ALU.add
                                        ).then_inc(gate_ready, 1)
                dve.wait_ge(gate_ready, b + 1)
                dve.wait_ge(xb_free, b + 2)
                for t in range(GT):
                    last = nc.vector.tensor_scalar(yb[:, t, :], yb[:, t, :], gate[:, t, 1:2], None, ALU.mult)
                last.then_inc(ybs_ready, 1)

            def read_attention(b):
                dve.wait_ge(e_used, b * PAIRS + (ER + PAIRS))
                nc.vector.tensor_scalar(e_sum[:, :], ps[:, 0:4, D], EPS_ATT, None, ALU.add).then_inc(esum_ready, 1)
                dve.wait_ge(esum_ready, b + 1)
                nc.vector.reciprocal(e_rsum[:, :], e_sum[:, :]).then_inc(ersum_ready, 1)
                dve.wait_ge(ersum_ready, b + 1)
                nc.vector.tensor_tensor(coef_a[:, :], e_rsum[:, :], gate[:, :, 0], ALU.mult).then_inc(coef_ready, 1)
                dve.wait_ge(coef_ready, b + 1)
                dve.wait_ge(ybs_ready, b + 1)
                for t in range(GT):
                    last = nc.vector.scalar_tensor_tensor(out=y_t[:, t, :], in0=ps[:, t, 0:D],
                                                          scalar=coef_a[:, t:t + 1], in1=yb[:, t, :],
                                                          op0=ALU.mult, op1=ALU.add)
                last.then_inc(xa_free, 1)

            def update_x(b):
                dve.wait_ge(yt_ready, b + 1)
                nc.vector.tensor_scalar(y_t, y_t, 0.5, 0.5, ALU.mult, ALU.add).then_inc(yh_ready, 1)
                dve.wait_ge(yh_ready, b + 1)
                nc.vector.tensor_tensor(y_t, x_sb[:, bass.ds(b * GT, GT), :], y_t, ALU.add).then_inc(x1_ready, 1)
                dve.wait_ge(x1_ready, b + 1)
                for t in range(GT):
                    nc.vector.bn_stats(stats[:, t, :], y_t[:, t, :]).then_inc(stats_d, 1)
                nc.vector.tensor_copy(x_sb[:, bass.ds(b * GT, GT), :], y_t).then_inc(x1_kept, 1)
                dve.wait_ge(mv_ready, b * GT + NT)
                dve.wait_ge(stats_d, b * GT + (NT + GT))
                nc.vector.memset(wait_cell[:, :], 0.0)
                for t in range(GT):
                    nc.vector.bn_aggr(mv_block[:, t, :], stats[:, t, :]).then_inc(mvb_ready, 1)
                dve.wait_ge(mvb_ready, b * GT + GT)
                nc.vector.tensor_copy(mean_var[:, bass.ds(b * GT, GT), :], mv_block[:, :, :]).then_inc(mv_ready, GT)

            def score_block(b, first, last):
                for p in range(PAIRS):
                    if not last or p + 2 < PAIRS:
                        leaky_relu(b, p + 2)
                    if not last or p + 1 < PAIRS:
                        mask_pair(b, p + 1)
                    score_lo(b, p)
                    if p == 3 and not first:
                        read_attention(b - 1)
                    if p == 4:
                        if not first:
                            update_x(b - 1)
                        read_gcn(b)
                    if p == 6:
                        apply_gate(b)

            leaky_relu(0, 0)
            leaky_relu(0, 1)
            mask_pair(0, 0)
            score_block(0, True, False)
            with dve.Fori(1, NG - 1) as b:
                score_block(b, False, False)
            score_block(NG - 1, False, True)

            normalise(NG)
            dve.wait_ge(w1_loaded, 48)
            nc.vector.tensor_copy(w1_hi[:, :, :], w1_raw[:, :, :]).then_inc(w1_hi_s, 1)
            dve.wait_ge(w1_hi_s, 1)
            nc.vector.tensor_tensor(w1_lo[:, :, :], w1_raw[:, :, :], w1_hi[:, :, :].bitcast(f32), ALU.subtract
                                    ).then_inc(w1_s, 1)
            relu_stage_lo(NG)
            read_attention(NG - 1)
            update_x(NG - 1)
            normalise(NG + 1)

            def add_bias(g):
                xs = x_sb[:, g * GT:(g + 1) * GT, :]
                dve.wait_ge(z_ready, NG + g + 1)
                nc.vector.tensor_tensor(xs, xs, bias_bc[:, :].unsqueeze(1).broadcast_to([P, GT, D]), ALU.add
                                        ).then_inc(xbias_ready, 1)

            for g in range(NG):
                for m in range(KD):
                    n = g * KD + m
                    dve.wait_ge(h1_hi, n + 1)
                    nc.vector.tensor_tensor(hh_lo[:, m, g * GN:(g + 1) * GN], ps[:, 6 + m, :],
                                            hh_hi[:, m, g * GN:(g + 1) * GN].bitcast(f32), ALU.subtract
                                            ).then_inc(h1_lo, 1)
                if g + 1 < NG:
                    relu_stage_lo(NG + g + 1)
                if g + 2 < NG:
                    normalise(NG + g + 2)
                for t in range(GT):
                    j = g * GT + t
                    dve.wait_ge(s1_hi, j + 1)
                    nc.vector.tensor_copy(v_sb[:, j:j + 1], ps[:, t, D:D + 1])
                    nc.vector.tensor_tensor(s_hl[:, j, 1, :], ps[:, t, 0:D], s_hl[:, j, 0, :].bitcast(f32),
                                            ALU.subtract).then_inc(s1_lo, 1)
                add_bias(g)
            dve.wait_ge(s1_lo, NT)
            nc.vector.tensor_reduce(v_max[:, :], v_sb[:, :], AX.X, ALU.max).then_inc(vmax_s, 1)
            dve.wait_ge(vgmax_s, 1)
            nc.vector.tensor_scalar(v_ngmax[:, :], v_gmax[:, :], -1.0, None, ALU.mult).then_inc(vneg_s, 1)

            def masked_half(i, s, h):
                dve.wait_ge(e_done, i * 2 + h + 1)
                dve.wait_ge(mask_ready, i + 1)
                if not (isinstance(i, int) and i == 0 and h == 0):
                    dve.wait_ge(em_ready, i * 2 + h)
                nc.vector.memset(wait_cell[:, :], 0.0)
                nc.vector.tensor_tensor_reduce(
                    out=em[:, s, h * 1024:(h + 1) * 1024], in0=ps[:, 2 * h:2 * h + 2, :],
                    in1=mask[:, s, h * 1024:(h + 1) * 1024].rearrange("p (a b) -> p a b", a=2),
                    scale=1.0, scalar=-3.0e38, op0=ALU.add, op1=ALU.max,
                    accum_out=row_max2[:, s, h:h + 1]).then_inc(em_ready, 1)

            def row_maximum(i, s):
                dve.wait_ge(em_ready, i * 2 + 2)
                nc.vector.tensor_reduce(neg_max[:, s:s + 1], row_max2[:, s, :], AX.X, ALU.max, negate=True
                                        ).then_inc(nmax_ready, 1)

            def transposed_lo(i, s, q):
                dve.wait_ge(pthi_ready, i * 4 + q + 1)
                nc.vector.tensor_tensor(pt_lo[:, s, 4 * q:4 * q + 4, :],
                                        ps[:, 4 + q % 2, :].rearrange("p (t c) -> p t c", t=4),
                                        pt_hi[:, s, 4 * q:4 * q + 4, :].bitcast(f32), ALU.subtract
                                        ).then_inc(ptlo_ready, 1)

            def finish_row(i, s, stored):
                dve.wait_ge(p_ready, i + 1)
                nc.vector.reciprocal(row_rsum[:, s:s + 1], row_sum[:, s:s + 1]).then_inc(rr_ready, 1)
                nc.vector.tensor_scalar(row_flag[:, s:s + 1], neg_max[:, s:s + 1], 0.5 * NEG_BIG,
                                        node_att[:, bass.ds(i, 1)], ALU.is_lt, ALU.mult).then_inc(rf_ready, 1)
                dve.wait_ge(rr_ready, i + 1)
                dve.wait_ge(rf_ready, i + 1)
                nc.vector.tensor_tensor(row_coef[:, s:s + 1], row_rsum[:, s:s + 1], row_flag[:, s:s + 1], ALU.mult
                                        ).then_inc(rc_ready, 1)
                dve.wait_ge(rc_ready, i + 1)
                dve.wait_ge(o_done, i + 1)
                if stored is not None:
                    dve.wait_ge(out_stored[s], stored)
                nc.vector.scalar_tensor_tensor(out=o_part[:, s, :], in0=ps[:, 6 + s, D:2 * D],
                                               scalar=row_coef[:, s:s + 1], in1=x_sb[:, bass.ds(i, 1), :].squeeze(1),
                                               op0=ALU.mult, op1=ALU.add).then_inc(op_ready, 1)
                dve.wait_ge(op_ready, i + 1)
                nc.vector.scalar_tensor_tensor(out=o_sb[:, s, :], in0=ps[:, 6 + s, 0:D],
                                               scalar=row_coef[:, s:s + 1], in1=o_part[:, s, :],
                                               op0=ALU.mult, op1=ALU.add).then_inc(o_ready, 1)

            def row_pair_step(i, s, stored):
                masked_half(i + 1, 1 - s, 0)
                transposed_lo(i, s, 0)
                transposed_lo(i, s, 1)
                masked_half(i + 1, 1 - s, 1)
                row_maximum(i + 1, 1 - s)
                transposed_lo(i, s, 2)
                transposed_lo(i, s, 3)
                finish_row(i, s, stored)

            masked_half(0, 0, 0)
            masked_half(0, 0, 1)
            row_maximum(0, 0)
            dve.wait_ge(vgsum_s, 1)
            nc.vector.reciprocal(v_rsum[:, :], v_gsum[:, :]).then_inc(vr_s, 1)
            dve.wait_ge(vr_s, 1)
            nc.vector.tensor_scalar(node_att[:, :], v_exp[:, :], v_rsum[:, 0:1], None, ALU.mult
                                    ).then_inc(natt_ready, 1)
            dve.wait_ge(natt_ready, 1)
            row_pair_step(0, 0, None)
            row_pair_step(1, 1, None)
            with dve.Fori(1, NT // 2 - 1) as i:
                for s in range(2):
                    row_pair_step(i * 2 + s, s, i * 16)
            row_pair_step(NT - 2, 0, 16 * (NT // 2 - 1))
            for q in range(4):
                transposed_lo(NT - 1, 1, q)
            finish_row(NT - 1, 1, 16 * (NT // 2 - 1))

        @block.tensor
        def _(pe):
            def transpose_group(n):
                tb = 0 if n < NG else 4
                pe.wait_ge(z_ready, n + 1)
                if n == 0:
                    pe.wait_ge(consts_ready, 1)
                if n == NG:
                    pe.wait_ge(xb_free, NG + 1)
                if n >= 1:
                    pe.wait_ge(sthi_ready, n)
                    pe.wait_ge(stlo_ready, n)
                for t in range(GT):
                    for k in range(KD):
                        last = nc.tensor.transpose(ps[:, tb + k, t * P:(t + 1) * P],
                                                   z_sb[:, n % ZR, t, k * P:(k + 1) * P], ident[:, :])
                last.then_inc(tr_done, 1)

            def stage(part, n, cols):
                return lambda k: part[:, n % 2, k, cols]

            transpose_group(0)
            for g in range(NG):
                pe.wait_ge(sthi_ready, g + 1)
                pe.wait_ge(stlo_ready, g + 1)
                if g == 0:
                    pe.wait_ge(wsplit, 1)
                if g + 1 < NG:
                    transpose_group(g + 1)
                every = slice(0, GN)
                if g >= 2:
                    pe.wait_ge(sl_ready, g - 1)
                three_products(ps[:, 6 + g % 2, :], lambda k: ul_hi[:, k, :], lambda k: ul_lo[:, k, :],
                               stage(stage_hi, g, every), stage(stage_lo, g, every)).then_inc(sl_done, 1)
                for t in range(GT):
                    j = g * GT + t
                    cols = slice(t * P, (t + 1) * P)
                    hi, lo = stage(stage_hi, g, cols), stage(stage_lo, g, cols)
                    if j >= 3:
                        pe.wait_ge(g_lo, j - 2)
                    three_products(ps[:, 2 + j % 3, :], hi, lo, lambda k: w0_hi[:, k, :], lambda k: w0_lo[:, k, :]
                                   ).then_inc(g_done, 1)
                    last = three_products(ps[:, 5, j * 6:(j + 1) * 6], hi, lo, lambda k: xc_hi[:, k, :],
                                          lambda k: xc_lo[:, k, :])
                last.then_inc(stage_used, 1)

            pe.wait_ge(ab_ready, 1)
            pe.wait_ge(sl_ready, NG)
            pe.wait_ge(g_lo, NT)
            with pe.Fori(0, NG) as b:
                pe.wait_ge(xb_free, b + 1)
                for j in range(NT):
                    if j % 4 == 0:
                        pe.wait_ge(adj_loaded[j // 4], b * 16 + 16)
                    for t in range(GT):
                        lhs = adj_ring[:, j, t * P:(t + 1) * P]
                        nc.tensor.matmul(ps[:, 4 + t, 0:DX], lhs, ab_hi[:, j, 1, :], start=(j == 0), stop=False)
                        last = nc.tensor.matmul(ps[:, 4 + t, 0:DX], lhs, ab_lo[:, j, 1, :], start=False,
                                                stop=(j == NT - 1))
                    if j % 4 == 3:
                        last.then_inc(adj_pe, 1)
                pe.wait_ge(xa_free, b + 1)
                for p in range(PAIRS):
                    pe.wait_ge(elo_ready, b * PAIRS + (EW + p + 1))
                    for h in range(2):
                        j = 2 * p + h
                        for t in range(GT):
                            cols = slice(t * P, (t + 1) * P)
                            hi, lo = e_hi[:, p % ER, h, cols], e_lo[:, p % ER, h, cols]
                            nc.tensor.matmul(ps[:, t, 0:DX], hi, ab_hi[:, j, 0, :], start=(j == 0), stop=False)
                            nc.tensor.matmul(ps[:, t, 0:D], hi, ab_lo[:, j, 0, 0:D], start=False, stop=False)
                            last = nc.tensor.matmul(ps[:, t, 0:DX], lo, ab_hi[:, j, 0, :], start=False,
                                                    stop=(j == NT - 1))
                    last.then_inc(e_used, 1)

            transpose_group(NG)
            pe.wait_ge(w1_s, 1)
            for g in range(NG):
                n = NG + g
                pe.wait_ge(sthi_ready, n + 1)
                pe.wait_ge(stlo_ready, n + 1)
                if g >= 1 and g + 1 < NG:
                    transpose_group(n + 1)
                every = slice(0, GN)
                for m in range(KD):
                    if g >= 1:
                        pe.wait_ge(h1_lo, (g - 1) * KD + m + 1)
                    rows = slice(m * P, (m + 1) * P)
                    three_products(ps[:, 6 + m, :], lambda k: w1_hi[:, k, rows], lambda k: w1_lo[:, k, rows],
                                   stage(stage_hi, n, every), stage(stage_lo, n, every)).then_inc(h1_done, 1)
                if g == 0:
                    transpose_group(n + 1)
                for t in range(GT):
                    if g == 0 and t == 0:
                        pe.wait_ge(xa_free, NG + 1)
                    if g >= 1:
                        pe.wait_ge(s1_lo, (g - 1) * GT + t + 1)
                    cols = slice(t * P, (t + 1) * P)
                    wide = slice(D, 2 * D + 2)
                    three_products(ps[:, t, 0:DX], stage(stage_hi, n, cols), stage(stage_lo, n, cols),
                                   lambda k: w1_hi[:, k, wide], lambda k: w1_lo[:, k, wide]).then_inc(s1_done, 1)

            def score_half(i, s, h, first):
                if not first:
                    pe.wait_ge(em_ready, i * 2 + (h - 1))
                for c in range(2 * h, 2 * h + 2):
                    cols = slice(c * GN, (c + 1) * GN)
                    last = three_products(ps[:, c, :], lambda k: hs_hi[:, s, k, :], lambda k: hs_lo[:, s, k, :],
                                          lambda k: hh_hi[:, k, cols], lambda k: hh_lo[:, k, cols])
                last.then_inc(e_done, 1)

            def transpose_quarter(i, s, q, first):
                if q >= 2 or not first:
                    pe.wait_ge(ptlo_ready, i * 4 + (q - 1))
                for t in range(4):
                    last = nc.tensor.transpose(ps[:, 4 + q % 2, t * P:(t + 1) * P],
                                               em[:, s, (4 * q + t) * P:(4 * q + t + 1) * P], ident[:, :])
                last.then_inc(t_done, 1)

            def row_products(i, s, first):
                if not first:
                    pe.wait_ge(o_ready, i - 1)
                for q in range(4):
                    pe.wait_ge(ptlo_ready, i * 4 + q + 1)
                    for j in range(4 * q, 4 * q + 4):
                        def hi_product():
                            return nc.tensor.matmul(ps[:, 6 + s, :], pt_hi[:, s, j, :], s_hl[:, j, :, :],
                                                    start=(j == 0), stop=(j == NT - 1))
                        if j == 0:
                            hi_product()
                        last = nc.tensor.matmul(ps[:, 6 + s, 0:D], pt_lo[:, s, j, :], s_hl[:, j, 0, :], start=False,
                                                stop=False)
                        if j > 0:
                            last = hi_product()
                last.then_inc(o_done, 1)

            def row_step(i, s, first, first_o):
                pe.wait_ge(hs_ready, i + 2)
                score_half(i + 1, 1 - s, 0, False)
                pe.wait_ge(p_ready, i + 1)
                transpose_quarter(i, s, 0, first)
                transpose_quarter(i, s, 1, first)
                score_half(i + 1, 1 - s, 1, False)
                transpose_quarter(i, s, 2, first)
                transpose_quarter(i, s, 3, first)
                row_products(i, s, first_o)

            pe.wait_ge(hs_ready, 1)
            pe.wait_ge(s1_lo, NT)
            score_half(0, 0, 0, True)
            score_half(0, 0, 1, True)
            row_step(0, 0, True, True)
            row_step(1, 1, False, True)
            with pe.Fori(1, NT // 2 - 1) as i:
                for s in range(2):
                    row_step(i * 2 + s, s, False, False)
            row_step(NT - 2, 0, False, False)
            pe.wait_ge(p_ready, NT)
            for q in range(4):
                transpose_quarter(NT - 1, 1, q, False)
            row_products(NT - 1, 1, False)


_INS = ["x", "adj", "adj_t", "L0_gnn_W_sa", "L0_gnn_a_sa", "L0_gnn_W_gcnb", "L0_gnn_b_gcnb", "L0_gnn_Wa", "L0_gnn_ba",
        "L0_gnn_Wb", "L0_gnn_bb", "L1_gnn_weight", "L1_gnn_bias", "L1_gnn_node_w", "L1_gnn_edge_w"]


def kernel(**inputs):
    import numpy as _np
    import concourse.bacc as _bacc
    from concourse import mybir as _mybir
    from concourse.bass_utils import run_bass_kernel_spmd as _run

    nc = _bacc.Bacc("TRN2", target_bir_lowering=False, num_devices=1)
    arrays, args = {}, []
    for name in _INS:
        a = _np.asarray(inputs["adj"]).T if name == "adj_t" else inputs[name]
        a = _np.ascontiguousarray(a)
        arrays[f"in_{name}_dram"] = a
        args.append(nc.dram_tensor(f"in_{name}_dram", a.shape, _mybir.dt.from_np(a.dtype), kind="ExternalInput").ap())
    x = arrays["in_x_dram"]
    args.append(nc.dram_tensor("out_0_dram", x.shape, _mybir.dt.from_np(x.dtype), kind="ExternalOutput").ap())
    build_two_graph_blocks(nc, *args)
    r = _run(nc, [arrays], core_ids=[0])
    return r.results[0]["out_0_dram"]
```

```python
import concourse.bass as bass
from concourse import mybir
from contextlib import ExitStack


def build_two_graph_blocks(nc: bass.Bass, x, adj, adj_t, W_sa, a_sa, W_gcnb, b_gcnb, Wa, ba, Wb, bb,
                           weight, bias, node_w, edge_w, out):
    f32, f32r = mybir.dt.float32, mybir.dt.float32r
    ALU = mybir.AluOpType
    ACT = mybir.ActivationFunctionType
    AX = mybir.AxisListType
    RED = bass.bass_isa.ReduceOp

    P = 128
    N, D = x.shape
    KD = D // P
    NT = N // P
    GT = 4
    GN = GT * P
    NG = N // GN
    PAIRS = NT // 2
    EW = 4
    ER = 4
    ZR = 3
    DX = D + 2
    DE = D + 4
    GCN_AFTER = [2, 4, 6, 7]
    SLOPE = 0.01
    NEG_BIG = 9.0e15
    F32_MAX = 3.0e38
    EPS_LN, EPS_ATT = 1e-5, 1e-5

    ctx = ExitStack()
    with ctx:
        def sb(name, shape, dt=f32, on=ctx):
            return on.enter_context(nc.sbuf_tensor(name, shape, dt))

        def sem(name):
            return ctx.enter_context(nc.semaphore(name))

        x_sb = sb("x_sb", [P, NT, D])
        z_sb = sb("z_sb", [P, ZR, GT, D])
        stage_hi = sb("stage_hi", [P, 2, KD, GN], f32r)
        stage_lo = sb("stage_lo", [P, 2, KD, GN], f32r)
        ident = sb("ident", [P, P])
        stats = sb("stats", [P, NT, 6])
        mean_var = sb("mean_var", [P, NT, 2])
        rstd = sb("rstd", [P, NT])
        minus_half = sb("minus_half", [P, NT])
        w1_raw = sb("w1_raw", [P, KD, 2 * D + 2])
        bgc_bc = sb("bgc_bc", [P, D])
        bias_bc = sb("bias_bc", [P, D])
        gate_bias = sb("gate_bias", [P, 2])
        wait_cell = sb("wait_cell", [P, 1])

        l0 = ExitStack()
        with l0:
            ab_hi = sb("ab_hi", [P, NT, 2, DE], f32r, l0)
            ab_lo = sb("ab_lo", [P, NT, 2, DE], f32r, l0)
            adj_ring = sb("adj_ring", [P, NT, GN], f32r, l0)
            e_hi = sb("e_hi", [P, ER, 2, GN], f32r, l0)
            e_lo = sb("e_lo", [P, ER, 2, GN], f32r, l0)
            sl_bc = sb("sl_bc", [P, N], f32, l0)
            s_right = sb("s_right", [P, NT], f32, l0)
            gate_x = sb("gate_x", [P, NT, 2], f32, l0)
            gate_z = sb("gate_z", [P, GT, 2], f32, l0)
            gate_t = sb("gate_t", [P, GT, 2], f32, l0)
            gate = sb("gate", [P, GT, 2], f32, l0)
            mv_block = sb("mv_block", [P, GT, 2], f32, l0)
            e_sum = sb("e_sum", [P, GT], f32, l0)
            e_rsum = sb("e_rsum", [P, GT], f32, l0)
            coef_a = sb("coef_a", [P, GT], f32, l0)
            yb, ya = z_sb[:, 0, :, :], z_sb[:, 2, :, :]
            y_end = z_sb[:, NG % ZR, :, :]
            w0 = ExitStack()
            with w0:
                w0_raw = sb("w0_raw", [P, KD, 2, DE], f32, w0)
                a_bc = sb("a_bc", [P, 2 * D], f32, w0)
                w0_hi = sb("w0_hi", [P, KD, 2, DE], f32r, w0)
                w0_lo = sb("w0_lo", [P, KD, 2, DE], f32r, w0)
                u_left = sb("u_left", [P, KD], f32, w0)
                ul_hi = sb("ul_hi", [P, KD, P], f32r, w0)
                ul_lo = sb("ul_lo", [P, KD, P], f32r, w0)
                u_junk = z_sb[:, 2, :, :]
            ew = sb("ew", [P, EW, 2, GN], f32, l0)

        hh_hi = sb("hh_hi", [P, KD, N], f32r)
        hh_lo = sb("hh_lo", [P, KD, N], f32r)
        s_hl = sb("s_hl", [P, NT, 2, D], f32r)
        w1_hi = sb("w1_hi", [P, KD, 2 * D + 2], f32r)
        w1_lo = sb("w1_lo", [P, KD, 2 * D + 2], f32r)
        mask = sb("mask", [P, 2, N])
        em = sb("em", [P, 2, N])
        pt_hi = sb("pt_hi", [P, 2, NT, P], f32r)
        pt_lo = sb("pt_lo", [P, 2, NT, P], f32r)
        hs_hi = sb("hs_hi", [P, 2, KD, P], f32r)
        hs_lo = sb("hs_lo", [P, 2, KD, P], f32r)
        row_max2 = sb("row_max2", [P, 2, 2])
        neg_max = sb("neg_max", [P, 2])
        row_sum = sb("row_sum", [P, 2])
        row_rsum = sb("row_rsum", [P, 2])
        row_flag = sb("row_flag", [P, 2])
        row_coef = sb("row_coef", [P, 2])
        o_part = sb("o_part", [P, 2, D])
        o_sb = sb("o_sb", [P, 2, D])
        v_sb = sb("v_sb", [P, NT])
        v_max = sb("v_max", [P, 1])
        v_gmax = sb("v_gmax", [P, 1])
        v_ngmax = sb("v_ngmax", [P, 1])
        v_exp = sb("v_exp", [P, NT])
        v_sum = sb("v_sum", [P, 1])
        v_gsum = sb("v_gsum", [P, 1])
        v_rsum = sb("v_rsum", [P, 1])
        node_att = sb("node_att", [P, NT])

        ps = ctx.enter_context(nc.psum_tensor("ps", [P, 8, GN], f32))

        x_loaded = [sem(f"x_loaded{g}") for g in range(NG)]
        cols_loaded = sem("cols_loaded")
        w0_loaded, w1_loaded, vec_loaded = sem("w0_loaded"), sem("w1_loaded"), sem("vec_loaded")
        consts_ready = sem("consts_ready")
        ident_z = sem("ident_z")
        stats_d = sem("stats_d")
        mv_ready = sem("mv_ready")
        ve_ready = sem("ve_ready")
        rstd_ready = sem("rstd_ready")
        u_ready, wsplit_hi, wsplit = sem("u_ready"), sem("wsplit_hi"), sem("wsplit")
        z_ready = sem("z_ready")
        tr_done = sem("tr_done")
        sthi_ready, stlo_ready = sem("sthi_ready"), sem("stlo_ready")
        g_done, g_hi, g_lo = sem("g_done"), sem("g_hi"), sem("g_lo")
        sl_done, sl_ready = sem("sl_done"), sem("sl_ready")
        sr_ready, gx_ready, ab_ready = sem("sr_ready"), sem("gx_ready"), sem("ab_ready")
        adj_loaded = [sem(f"adj_loaded{g}") for g in range(4)]
        adj_pe = sem("adj_pe")
        ew_s, ew_z, ew_x, ew_m = sem("ew_s"), sem("ew_z"), sem("ew_x"), sem("ew_m")
        ehi_ready = sem("ehi_ready")
        elo_ready = sem("elo_ready")
        e_used = sem("e_used")
        xb_free, xa_free = sem("xb_free"), sem("xa_free")
        gz_ready, gt_ready, gate_ready = sem("gz_ready"), sem("gt_ready"), sem("gate_ready")
        yb_ready, esum_ready, ersum_ready, coef_ready = (sem("yb_ready"), sem("esum_ready"),
                                                         sem("ersum_ready"), sem("coef_ready"))
        y_ready, yt_ready, x1_ready = sem("y_ready"), sem("yt_ready"), sem("x1_ready")
        x1_kept, mvb_ready = sem("x1_kept"), sem("mvb_ready")
        w1_hi_s, w1_s = sem("w1_hi_s"), sem("w1_s")
        xbias_ready = sem("xbias_ready")
        h1_done, h1_hi, h1_lo = sem("h1_done"), sem("h1_hi"), sem("h1_lo")
        s1_done, s1_hi, s1_lo, v_ready = sem("s1_done"), sem("s1_hi"), sem("s1_lo"), sem("v_ready")
        vmax_s, vgmax_s, vneg_s, vexp_s, vgsum_s, vr_s, natt_ready = (
            sem("vmax_s"), sem("vgmax_s"), sem("vneg_s"), sem("vexp_s"), sem("vgsum_s"), sem("vr_s"),
            sem("natt_ready"))
        mask_loaded = [sem("mask_loaded0"), sem("mask_loaded1")]
        mask_ready = sem("mask_ready")
        hs_ready = sem("hs_ready")
        e_done = sem("e_done")
        em_ready = sem("em_ready")
        nmax_ready, p_ready = sem("nmax_ready"), sem("p_ready")
        t_done = sem("t_done")
        pthi_ready, ptlo_ready = sem("pthi_ready"), sem("ptlo_ready")
        o_done, op_ready, o_ready = sem("o_done"), sem("op_ready"), sem("o_ready")
        rr_ready, rf_ready, rc_ready = sem("rr_ready"), sem("rf_ready"), sem("rc_ready")
        out_stored = [sem("out_stored0"), sem("out_stored1")]

        xg = x.rearrange("(g t p) d -> g p t d", t=GT, p=P)
        adjt_v = adj_t.rearrange("(q t p) n -> q p t n", q=4, p=P)
        adj_v = adj.rearrange("(t p) n -> t p n", p=P)
        out_v = out.rearrange("(t p) d -> t p d", p=P)

        def z_rows(n):
            if n < NG + 2:
                return z_sb[:, n % ZR, :, :]
            return em[:, n % 2, 0:GT * D].rearrange("p (t d) -> p t d", t=GT)

        def kview(w):
            return w.rearrange("(k p) c -> p k c", p=P)

        def three_products(pe_out, lhs_hi, lhs_lo, rhs_hi, rhs_lo):
            terms = [(lhs_hi, rhs_hi), (lhs_hi, rhs_lo), (lhs_lo, rhs_hi)]
            for n, (a, b) in enumerate(terms):
                for k in range(KD):
                    last = nc.tensor.matmul(pe_out, a(k), b(k), start=(n == 0 and k == 0),
                                            stop=(n == 2 and k == KD - 1))
            return last

        block = ctx.enter_context(nc.Block())

        @block.sync
        def _(sp):
            for g in range(NG):
                sp.dma_start(x_sb[:, g * GT:(g + 1) * GT, :], xg[g]).then_inc(x_loaded[g], 16)
                if g == 0:
                    sp.dma_start(w0_raw[:, :, 0, 0:D], kview(W_sa)).then_inc(w0_loaded, 16)
                    sp.dma_start(a_bc[:, :], a_sa[0].partition_broadcast(P)).then_inc(w0_loaded, 16)
                    sp.dma_start(w0_raw[:, :, 1, 0:D], kview(W_gcnb)).then_inc(w0_loaded, 16)
            sp.dma_start(bgc_bc[:, :], b_gcnb.partition_broadcast(P)).then_inc(vec_loaded, 16)
            sp.dma_start(bias_bc[:, :], bias.partition_broadcast(P)).then_inc(vec_loaded, 16)
            sp.dma_start(gate_bias[:, 0:1], ba.partition_broadcast(P)).then_inc(vec_loaded, 16)
            sp.dma_start(gate_bias[:, 1:2], bb.partition_broadcast(P)).then_inc(vec_loaded, 16)
            sp.dma_start(w1_raw[:, :, 0:D], kview(edge_w)).then_inc(w1_loaded, 16)
            sp.dma_start(w1_raw[:, :, D:2 * D], kview(weight)).then_inc(w1_loaded, 16)
            sp.dma_start(w1_raw[:, :, 2 * D:2 * D + 1], kview(node_w),
                         allow_slow_non_contiguous=True).then_inc(w1_loaded, 16)

            sp.wait_ge(e_used, ER + NG * PAIRS)
            sp.wait_ge(x1_kept, NG)
            for t in range(2):
                sp.dma_start(mask[:, t, :], adj_v[t]).then_inc(mask_loaded[t], 16)
            with sp.Fori(0, NT // 2 - 1) as i:
                for s in range(2):
                    sp.wait_ge(em_ready, i * 4 + 2 * s + 2)
                    sp.dma_start(mask[:, s, :], adj_v[i * 2 + s + 2]).then_inc(mask_loaded[s], 16)
                for s in range(2):
                    sp.wait_ge(o_ready, i * 2 + s + 1)
                    sp.dma_start(out_v[i * 2 + s], o_sb[:, s, :]).then_inc(out_stored[s], 16)
            for s in range(2):
                sp.wait_ge(o_ready, NT - 1 + s)
                sp.dma_start(out_v[NT - 2 + s], o_sb[:, s, :]).then_inc(out_stored[s], 16)
            for s in range(2):
                sp.wait_ge(out_stored[s], 16 * (NT // 2))

        @block.gpsimd
        def _(pool):
            def load_adj_quarter(b, q):
                pool.dma_start(adj_ring[:, q * 4:(q + 1) * 4, :],
                               adjt_v[q][:, :, bass.ds(b * GN, GN)]).then_inc(adj_loaded[q], 16)

            nc.gpsimd.memset(ident[:, :], 0.0).then_inc(ident_z, 1)
            nc.gpsimd.memset(minus_half[:, :], -0.5)
            nc.gpsimd.memset(w0_raw[:, :, 0, D:DX], 0.0)
            nc.gpsimd.memset(w0_raw[:, :, 0, DX + 1:DE], 0.0)
            nc.gpsimd.memset(w1_raw[:, :, 2 * D + 1:2 * D + 2], 0.0)
            pool.wait_ge(ident_z, 1)
            nc.gpsimd.affine_select(out=ident[:, :], in_=ident[:, :], compare_op=ALU.not_equal, fill=1.0, base=0,
                                    pattern=[[-1, P]], channel_multiplier=1).then_inc(consts_ready, 1)
            def group_rstd(n):
                g = n % NG
                sl = slice(g * GT, (g + 1) * GT)
                pool.wait_ge(mv_ready, GT * (n + 1))
                if n >= NG:
                    pool.wait_ge(z_ready, g + 1)
                nc.gpsimd.tensor_scalar(rstd[:, sl], mean_var[:, sl, 1], EPS_LN, None, ALU.add).then_inc(ve_ready, 1)
                pool.wait_ge(ve_ready, n + 1)
                nc.gpsimd.tensor_tensor(rstd[:, sl], rstd[:, sl], minus_half[:, sl], ALU.pow
                                        ).then_inc(rstd_ready, 1)

            for g in range(NG):
                group_rstd(g)
                load_adj_quarter(0, g)
            with pool.Fori(1, NG) as b:
                for q in range(4):
                    pool.wait_ge(adj_pe, b * 4 + (q + 1 - 4))
                    pool.wait_ge(ew_m, b * PAIRS + (2 * q + 2 - PAIRS))
                    load_adj_quarter(b, q)
            for g in range(NG):
                group_rstd(NG + g)
            pool.wait_ge(vec_loaded, 64)
            nc.gpsimd.tensor_scalar(bias_bc[:, :], bias_bc[:, :], 0.5, None, ALU.add).then_inc(xbias_ready, 1)
            pool.wait_ge(xbias_ready, 1)
            for g in range(NG):
                xs = x_sb[:, g * GT:(g + 1) * GT, :]
                pool.wait_ge(z_ready, NG + g + 1)
                if g == NG - 1:
                    pool.wait_ge(x1_kept, NG)
                nc.gpsimd.tensor_tensor(xs, xs, bias_bc[:, :].unsqueeze(1).broadcast_to([P, GT, D]), ALU.add
                                        ).then_inc(xbias_ready, 1)
            def stage_row(i, s):
                nc.gpsimd.tensor_copy(hs_hi[:, s, :, :], hh_hi[:, :, bass.ds(i * P, P)].bitcast(f32))
                nc.gpsimd.tensor_copy(hs_lo[:, s, :, :], hh_lo[:, :, bass.ds(i * P, P)].bitcast(f32)
                                      ).then_inc(hs_ready, 1)
            pool.wait_ge(h1_hi, 2 * NG)
            pool.wait_ge(h1_lo, 2 * NG)
            stage_row(2, 0)
            stage_row(3, 1)
            pool.wait_ge(vmax_s, 1)
            nc.gpsimd.partition_all_reduce(v_gmax[:, :], v_max[:, :], P, RED.max).then_inc(vgmax_s, 1)
            pool.wait_ge(vexp_s, 1)
            nc.gpsimd.partition_all_reduce(v_gsum[:, :], v_sum[:, :], P, RED.add).then_inc(vgsum_s, 1)
            with pool.Fori(2, NT // 2) as i:
                for s in range(2):
                    pool.wait_ge(e_done, i * 4 + (2 * s + 2 - 4))
                    stage_row(i * 2 + s, s)

        @block.scalar
        def _(act):
            def relu_stage(n):
                act.wait_ge(tr_done, n + 1)
                if 2 <= n < NG + 2:
                    act.wait_ge(g_done, GT * min(n - 1, NG))
                if n >= NG + 2:
                    act.wait_ge(s1_done, GT * (n - NG - 1))
                tb = 0 if n < NG else 4
                nc.scalar.activation(stage_hi[:, n % 2, :, :], ps[:, tb:tb + 2, :], ACT.Relu).then_inc(sthi_ready, 1)

            for side in range(2):
                for c, w in enumerate((Wa, Wb)):
                    col = D + 2 * side + c
                    act.dma_start(w0_raw[:, :, 1, col:col + 1],
                                  w[0:1, side * D:(side + 1) * D].rearrange("o (k p) -> p k o", p=P),
                                  allow_slow_non_contiguous=True).then_inc(cols_loaded, 16)

            act.wait_ge(consts_ready, 1)
            act.wait_ge(cols_loaded, 4 * 16)
            act.wait_ge(w0_loaded, 3 * 16)
            act.wait_ge(u_ready, 2 * KD)
            nc.scalar.copy(ul_hi[:, :, :], u_left[:, :].unsqueeze(2).broadcast_to([P, KD, P]))
            nc.scalar.copy(w0_hi[:, :, :, :], w0_raw[:, :, :, :]).then_inc(wsplit_hi, 1)
            relu_stage(0)
            for g in range(NG):
                act.wait_ge(sl_done, g + 1)
                nc.scalar.copy(sl_bc[:, g * GN:(g + 1) * GN], ps[:, 6 + g % 2, :]).then_inc(sl_ready, 1)
                for t in range(GT):
                    if t == 2 and g + 1 < NG:
                        relu_stage(g + 1)
                    j = g * GT + t
                    act.wait_ge(g_done, j + 1)
                    b0 = 2 + 2 * (j % 2)
                    nc.scalar.copy(ab_hi[:, j, :, :], ps[:, b0:b0 + 2, 0:DE]).then_inc(g_hi, 1)

            def score_sum(b, p):
                if p >= PAIRS:
                    b, p = b + 1, p - PAIRS
                for h in range(2):
                    last = nc.scalar.activation(ew[:, p % EW, h, :], sl_bc[:, bass.ds(b * GN, GN)], ACT.Identity,
                                                bias=s_right[:, 2 * p + h:2 * p + h + 1])
                last.then_inc(ew_s, 1)

            def score_exp(b, p):
                act.wait_ge(ew_z, b * PAIRS + p + 1)
                w = ew[:, p % EW, :, :]
                nc.scalar.activation(w, w, ACT.Exp, scale=-1.0).then_inc(ew_x, 1)

            def score_hi(b, p):
                act.wait_ge(ew_m, b * PAIRS + p + 1)
                act.wait_ge(e_used, b * PAIRS + p + 1)
                nc.scalar.copy(e_hi[:, p % ER, :, :], ew[:, p % EW, :, :]).then_inc(ehi_ready, 1)

            def score_block(b, first, last):
                for p in range(PAIRS):
                    if not last or p + 2 < PAIRS:
                        if not first or p + 2 >= EW:
                            act.wait_ge(elo_ready, b * PAIRS + p + 3)
                        score_exp(b, p + 1)
                        score_sum(b, p + 2)
                    elif p + 1 < PAIRS:
                        score_exp(b, p + 1)
                    if p == ER - 1 and not first:
                        attention_part(b - 1, ya)
                    score_hi(b, p)
                    if p == 4:
                        if not first:
                            y_tanh(b - 1, ya)
                        act.wait_ge(gz_ready, b + 1)
                        nc.scalar.activation(gate_t[:, :, :], gate_z[:, :, :], ACT.Tanh, scale=0.5
                                             ).then_inc(gt_ready, 1)
                    if p == 6 and not first:
                        keep_x1(b - 1, ya)

            def attention_part(b, y):
                act.wait_ge(coef_ready, b + 1)
                for t in range(GT):
                    last = nc.scalar.activation(y[:, t, :], ps[:, t, 0:D], ACT.Copy, scale=coef_a[:, t:t + 1])
                last.then_inc(xa_free, 1)

            def y_tanh(b, y):
                act.wait_ge(y_ready, b + 1)
                nc.scalar.activation(y, y, ACT.Tanh, scale=0.5).then_inc(yt_ready, 1)

            def keep_x1(b, y):
                act.wait_ge(x1_ready, b + 1)
                nc.scalar.copy(x_sb[:, bass.ds(b * GT, GT), :], y).then_inc(x1_kept, 1)

            act.wait_ge(sr_ready, 1)
            act.wait_ge(sl_ready, NG)
            score_sum(0, 0)
            score_sum(0, 1)
            score_exp(0, 0)
            score_block(0, True, False)
            with act.Fori(1, NG - 1) as b:
                score_block(b, False, False)
            score_block(NG - 1, False, True)
            relu_stage(NG)
            act.wait_ge(w1_loaded, 48)
            nc.scalar.copy(w1_hi[:, :, :], w1_raw[:, :, :]).then_inc(w1_hi_s, 1)
            act.wait_ge(tr_done, NG + 1)
            attention_part(NG - 1, y_end)

            for g in range(NG):
                for m in range(KD):
                    n = g * KD + m
                    act.wait_ge(h1_done, n + 1)
                    nc.scalar.copy(hh_hi[:, m, g * GN:(g + 1) * GN], ps[:, 6 + m, :]).then_inc(h1_hi, 1)
                if g < NG - 1:
                    relu_stage(NG + g + 1)
                if g == 0:
                    y_tanh(NG - 1, y_end)
                for t in range(GT):
                    j = g * GT + t
                    act.wait_ge(s1_done, j + 1)
                    nc.scalar.copy(s_hl[:, j, 0, :], ps[:, t, 0:D]).then_inc(s1_hi, 1)
                if g == 0:
                    keep_x1(NG - 1, y_end)

            def make_mask(s, n):
                act.wait_ge(mask_loaded[s], n)
                nc.scalar.activation(mask[:, s, :], mask[:, s, :], ACT.Copy, bias=-NEG_BIG, scale=NEG_BIG
                                     ).then_inc(mask_ready, 1)

            def exp_row(i, s):
                act.wait_ge(nmax_ready, i + 1)
                nc.scalar.activation(em[:, s, :], em[:, s, :], ACT.Exp, bias=neg_max[:, s:s + 1],
                                     accum_out=row_sum[:, s:s + 1]).then_inc(p_ready, 1)

            def transposed_hi(i, s, q):
                act.wait_ge(t_done, i * 4 + q + 1)
                nc.scalar.copy(pt_hi[:, s, 4 * q:4 * q + 4, :],
                               ps[:, 4 + q % 2, :].rearrange("p (t c) -> p t c", t=4)).then_inc(pthi_ready, 1)

            make_mask(0, 16)
            make_mask(1, 16)
            exp_row(0, 0)
            act.wait_ge(vneg_s, 1)
            nc.scalar.activation(v_exp[:, :], v_sb[:, :], ACT.Exp, bias=v_ngmax[:, 0:1],
                                 accum_out=v_sum[:, :]).then_inc(vexp_s, 1)
            with act.Fori(0, NT // 2 - 1) as i:
                for s in range(2):
                    for q in range(4):
                        transposed_hi(i * 2 + s, s, q)
                    make_mask(s, i * 16 + 32)
                    exp_row(i * 2 + s + 1, 1 - s)
            for s in range(2):
                for q in range(4):
                    transposed_hi(NT - 2 + s, s, q)
                if s == 0:
                    exp_row(NT - 1, 1)

        @block.vector
        def _(dve):
            dve.sem_inc(elo_ready, EW)
            dve.sem_inc(e_used, ER)
            dve.sem_inc(xb_free, 1)
            dve.sem_inc(xa_free, 1)

            def group_stats(g):
                dve.wait_ge(x_loaded[g], 16)
                for j in range(g * GT, (g + 1) * GT):
                    nc.vector.bn_stats(stats[:, j, :], x_sb[:, j, :]).then_inc(stats_d, 1)
                for j in range(g * GT, (g + 1) * GT):
                    dve.wait_ge(stats_d, j + 1)
                    nc.vector.bn_aggr(mean_var[:, j, :], stats[:, j, :]).then_inc(mv_ready, 1)

            def normalise(n):
                g = n % NG
                rows = y_end if n == 2 * NG - 1 else x_sb[:, g * GT:(g + 1) * GT, :]
                dve.wait_ge(rstd_ready, n + 1)
                if ZR <= n < NG + 2:
                    dve.wait_ge(tr_done, n - ZR + 1)
                for t in range(GT):
                    j = g * GT + t
                    last = nc.vector.tensor_scalar(z_rows(n)[:, t, :], rows[:, t, :], mean_var[:, j, 0:1],
                                                   rstd[:, j:j + 1], ALU.subtract, ALU.mult)
                last.then_inc(z_ready, 1)

            def relu_stage_lo(n):
                dve.wait_ge(sthi_ready, n + 1)
                tb = 0 if n < NG else 4
                nc.vector.scalar_tensor_tensor(out=stage_lo[:, n % 2, :, :], in0=ps[:, tb:tb + 2, :], scalar=0.0,
                                               in1=stage_hi[:, n % 2, :, :].bitcast(f32), op0=ALU.max,
                                               op1=ALU.subtract).then_inc(stlo_ready, 1)

            def score_weights():
                dve.wait_ge(w0_loaded, 3 * 16)
                for k in range(KD):
                    for side, dst in enumerate((u_left[:, k:k + 1], w0_raw[:, k, 0, DX:DX + 1])):
                        nc.vector.tensor_tensor_reduce(out=u_junk[:, 2 * k + side, :], in0=w0_raw[:, k, 0, 0:D],
                                                       in1=a_bc[:, side * D:(side + 1) * D], scale=1.0, scalar=0.0,
                                                       op0=ALU.mult, op1=ALU.add, accum_out=dst).then_inc(u_ready, 1)

            def split_weights_lo():
                dve.wait_ge(u_ready, 2 * KD)
                ul_b = u_left[:, :].unsqueeze(2).broadcast_to([P, KD, P])
                dve.wait_ge(wsplit_hi, 1)
                nc.vector.tensor_tensor(ul_lo[:, :, :], ul_b, ul_hi[:, :, :].bitcast(f32), ALU.subtract)
                nc.vector.tensor_tensor(w0_lo[:, :, :, :], w0_raw[:, :, :, :], w0_hi[:, :, :, :].bitcast(f32),
                                        ALU.subtract).then_inc(wsplit, 1)

            group_stats(0)
            score_weights()
            normalise(0)
            split_weights_lo()
            relu_stage_lo(0)
            group_stats(1)
            normalise(1)
            group_stats(2)
            for g in range(NG):
                for t in range(GT):
                    if t == 2 and g + 1 < NG:
                        relu_stage_lo(g + 1)
                    j = g * GT + t
                    dve.wait_ge(g_hi, j + 1)
                    b0 = 2 + 2 * (j % 2)
                    nc.vector.tensor_tensor(ab_lo[:, j, :, :], ps[:, b0:b0 + 2, 0:DE],
                                            ab_hi[:, j, :, :].bitcast(f32), ALU.subtract).then_inc(g_lo, 1)
                    if t == 2 and g + 2 < NG:
                        normalise(g + 2)
                    if t == 3 and g + 3 < NG:
                        group_stats(g + 3)

            dve.wait_ge(g_lo, NT)
            nc.vector.tensor_tensor(s_right[:, :], ab_hi[:, :, 0, DX].bitcast(f32), ab_lo[:, :, 0, DX].bitcast(f32),
                                    ALU.add).then_inc(sr_ready, 1)
            nc.vector.tensor_tensor(gate_x[:, :, :], ab_hi[:, :, 1, DX:DE].bitcast(f32),
                                    ab_lo[:, :, 1, DX:DE].bitcast(f32), ALU.add).then_inc(gx_ready, 1)
            nc.vector.memset(ab_hi[:, :, 0, D:D + 1].bitcast(f32), 1.0).then_inc(ab_ready, 1)
            dve.wait_ge(vec_loaded, 64)
            dve.wait_ge(gx_ready, 1)
            nc.vector.tensor_tensor(gate_x[:, :, :], gate_x[:, :, :],
                                    gate_bias[:, :].unsqueeze(1).broadcast_to([P, NT, 2]), ALU.add
                                    ).then_inc(ab_ready, 1)
            dve.wait_ge(ab_ready, 2)

            def leaky_relu(b, p):
                if p >= PAIRS:
                    b, p = b + 1, p - PAIRS
                dve.wait_ge(ew_s, b * PAIRS + p + 1)
                w = ew[:, p % EW, :, :]
                nc.vector.scalar_tensor_tensor(out=w, in0=w, scalar=SLOPE, in1=w, op0=ALU.mult, op1=ALU.max
                                               ).then_inc(ew_z, 1)

            def mask_pair(b, p):
                if p >= PAIRS:
                    b, p = b + 1, p - PAIRS
                if p % 2 == 0:
                    dve.wait_ge(adj_loaded[p // 2], b * 16 + 16)
                dve.wait_ge(ew_x, b * PAIRS + p + 1)
                w = ew[:, p % EW, :, :]
                nc.vector.scalar_tensor_tensor(out=w, in0=w, scalar=F32_MAX,
                                               in1=adj_ring[:, 2 * p:2 * p + 2, :].bitcast(f32), op0=ALU.min,
                                               op1=ALU.mult).then_inc(ew_m, 1)

            def score_lo(b, p):
                dve.wait_ge(ehi_ready, b * PAIRS + p + 1)
                nc.vector.tensor_tensor(e_lo[:, p % ER, :, :], ew[:, p % EW, :, :],
                                        e_hi[:, p % ER, :, :].bitcast(f32), ALU.subtract).then_inc(elo_ready, 1)

            def read_gcn(b):
                dve.wait_ge(adj_pe, b * 4 + 4)
                nc.vector.tensor_tensor(gate_z[:, :, :], ps[:, 4:8, D:DX], gate_x[:, bass.ds(b * GT, GT), :], ALU.add
                                        ).then_inc(gz_ready, 1)
                nc.vector.tensor_tensor(yb, ps[:, 4:8, 0:D], bgc_bc[:, :].unsqueeze(1).broadcast_to([P, GT, D]),
                                        ALU.add).then_inc(xb_free, 1)

            def make_gates(b):
                dve.wait_ge(gt_ready, b + 1)
                nc.vector.tensor_scalar(gate[:, :, :], gate_t[:, :, :], 0.5, 0.5, ALU.mult, ALU.add
                                        ).then_inc(gate_ready, 1)

            def attention_coefs(b):
                dve.wait_ge(e_used, b * PAIRS + (ER + PAIRS))
                dve.wait_ge(gate_ready, b + 1)
                nc.vector.tensor_scalar(e_sum[:, :], ps[:, 0:4, D], EPS_ATT, None, ALU.add).then_inc(esum_ready, 1)
                dve.wait_ge(esum_ready, b + 1)
                nc.vector.reciprocal(e_rsum[:, :], e_sum[:, :]).then_inc(ersum_ready, 1)
                dve.wait_ge(ersum_ready, b + 1)
                nc.vector.tensor_tensor(coef_a[:, :], e_rsum[:, :], gate[:, :, 0], ALU.mult).then_inc(coef_ready, 1)

            def make_y(b, y):
                dve.wait_ge(xa_free, b + 2)
                for t in range(GT):
                    last = nc.vector.scalar_tensor_tensor(out=y[:, t, :], in0=yb[:, t, :], scalar=gate[:, t, 1:2],
                                                          in1=y[:, t, :], op0=ALU.mult, op1=ALU.add)
                last.then_inc(y_ready, 1)

            def update_x(b, y):
                dve.wait_ge(yt_ready, b + 1)
                nc.vector.scalar_tensor_tensor(out=y, in0=y, scalar=0.5, in1=x_sb[:, bass.ds(b * GT, GT), :],
                                               op0=ALU.mult, op1=ALU.add).then_inc(x1_ready, 1)

            def x1_stats(b, y):
                dve.wait_ge(x1_ready, b + 1)
                for t in range(GT):
                    nc.vector.bn_stats(stats[:, t, :], y[:, t, :]).then_inc(stats_d, 1)
                dve.wait_ge(mv_ready, b * GT + NT)
                dve.wait_ge(stats_d, b * GT + (NT + GT))
                nc.vector.memset(wait_cell[:, :], 0.0)
                for t in range(GT):
                    nc.vector.bn_aggr(mv_block[:, t, :], stats[:, t, :]).then_inc(mvb_ready, 1)
                dve.wait_ge(mvb_ready, b * GT + GT)
                nc.vector.tensor_copy(mean_var[:, bass.ds(b * GT, GT), :], mv_block[:, :, :]).then_inc(mv_ready, GT)

            def score_block(b, first, last):
                for p in range(PAIRS):
                    if p == ER - 1 and not first:
                        attention_coefs(b - 1)
                    if not last or p + 2 < PAIRS:
                        leaky_relu(b, p + 2)
                    if not last or p + 1 < PAIRS:
                        mask_pair(b, p + 1)
                    score_lo(b, p)
                    if p == ER - 1:
                        if not first:
                            make_y(b - 1, ya)
                            dve.wait_ge(y_ready, b)
                        read_gcn(b)
                    if p == 5 and not first:
                        update_x(b - 1, ya)
                    if p == 6:
                        make_gates(b)
                        if not first:
                            x1_stats(b - 1, ya)
                        if last:
                            normalise(NG)

            leaky_relu(0, 0)
            leaky_relu(0, 1)
            mask_pair(0, 0)
            score_block(0, True, False)
            with dve.Fori(1, NG - 1) as b:
                score_block(b, False, False)
            score_block(NG - 1, False, True)

            relu_stage_lo(NG)
            dve.wait_ge(w1_hi_s, 1)
            nc.vector.tensor_tensor(w1_lo[:, :, :], w1_raw[:, :, :], w1_hi[:, :, :].bitcast(f32), ALU.subtract
                                    ).then_inc(w1_s, 1)
            dve.wait_ge(x1_kept, NG - 1)
            normalise(NG + 1)
            attention_coefs(NG - 1)
            normalise(NG + 2)
            make_y(NG - 1, y_end)

            for g in range(NG):
                for m in range(KD):
                    n = g * KD + m
                    if m == KD - 1 and g < NG - 1:
                        relu_stage_lo(NG + g + 1)
                    dve.wait_ge(h1_hi, n + 1)
                    nc.vector.tensor_tensor(hh_lo[:, m, g * GN:(g + 1) * GN], ps[:, 6 + m, :],
                                            hh_hi[:, m, g * GN:(g + 1) * GN].bitcast(f32), ALU.subtract
                                            ).then_inc(h1_lo, 1)
                if g == 0:
                    update_x(NG - 1, y_end)
                    x1_stats(NG - 1, y_end)
                if g == 1:
                    normalise(2 * NG - 1)
                for t in range(GT):
                    j = g * GT + t
                    dve.wait_ge(s1_hi, j + 1)
                    nc.vector.tensor_copy(v_sb[:, j:j + 1], ps[:, t, D:D + 1])
                    nc.vector.tensor_tensor(s_hl[:, j, 1, :], ps[:, t, 0:D], s_hl[:, j, 0, :].bitcast(f32),
                                            ALU.subtract).then_inc(s1_lo, 1)
            dve.wait_ge(s1_lo, NT)
            nc.vector.tensor_reduce(v_max[:, :], v_sb[:, :], AX.X, ALU.max).then_inc(vmax_s, 1)

            def masked_half(i, s, h):
                dve.wait_ge(e_done, i * 2 + h + 1)
                dve.wait_ge(mask_ready, i + 1)
                if not (isinstance(i, int) and i == 0 and h == 0):
                    dve.wait_ge(em_ready, i * 2 + h)
                nc.vector.memset(wait_cell[:, :], 0.0)
                nc.vector.tensor_tensor_reduce(
                    out=em[:, s, h * 1024:(h + 1) * 1024], in0=ps[:, 2 * h:2 * h + 2, :],
                    in1=mask[:, s, h * 1024:(h + 1) * 1024].rearrange("p (a b) -> p a b", a=2),
                    scale=1.0, scalar=-3.0e38, op0=ALU.add, op1=ALU.max,
                    accum_out=row_max2[:, s, h:h + 1]).then_inc(em_ready, 1)

            def row_maximum(i, s):
                dve.wait_ge(em_ready, i * 2 + 2)
                nc.vector.tensor_reduce(neg_max[:, s:s + 1], row_max2[:, s, :], AX.X, ALU.max, negate=True
                                        ).then_inc(nmax_ready, 1)

            def transposed_lo(i, s, q):
                dve.wait_ge(pthi_ready, i * 4 + q + 1)
                nc.vector.tensor_tensor(pt_lo[:, s, 4 * q:4 * q + 4, :],
                                        ps[:, 4 + q % 2, :].rearrange("p (t c) -> p t c", t=4),
                                        pt_hi[:, s, 4 * q:4 * q + 4, :].bitcast(f32), ALU.subtract
                                        ).then_inc(ptlo_ready, 1)

            def finish_row(i, s, stored):
                dve.wait_ge(p_ready, i + 1)
                nc.vector.reciprocal(row_rsum[:, s:s + 1], row_sum[:, s:s + 1]).then_inc(rr_ready, 1)
                nc.vector.tensor_scalar(row_flag[:, s:s + 1], neg_max[:, s:s + 1], 0.5 * NEG_BIG,
                                        node_att[:, bass.ds(i, 1)], ALU.is_lt, ALU.mult).then_inc(rf_ready, 1)
                dve.wait_ge(rr_ready, i + 1)
                dve.wait_ge(rf_ready, i + 1)
                nc.vector.tensor_tensor(row_coef[:, s:s + 1], row_rsum[:, s:s + 1], row_flag[:, s:s + 1], ALU.mult
                                        ).then_inc(rc_ready, 1)
                dve.wait_ge(rc_ready, i + 1)
                dve.wait_ge(o_done, i + 1)
                if stored is not None:
                    dve.wait_ge(out_stored[s], stored)
                nc.vector.scalar_tensor_tensor(out=o_part[:, s, :], in0=ps[:, 6 + s, D:2 * D],
                                               scalar=row_coef[:, s:s + 1], in1=x_sb[:, bass.ds(i, 1), :].squeeze(1),
                                               op0=ALU.mult, op1=ALU.add).then_inc(op_ready, 1)
                dve.wait_ge(op_ready, i + 1)
                nc.vector.scalar_tensor_tensor(out=o_sb[:, s, :], in0=ps[:, 6 + s, 0:D],
                                               scalar=row_coef[:, s:s + 1], in1=o_part[:, s, :],
                                               op0=ALU.mult, op1=ALU.add).then_inc(o_ready, 1)

            def node_attention():
                dve.wait_ge(vgsum_s, 1)
                nc.vector.reciprocal(v_rsum[:, :], v_gsum[:, :]).then_inc(vr_s, 1)
                dve.wait_ge(vr_s, 1)
                nc.vector.tensor_scalar(node_att[:, :], v_exp[:, :], v_rsum[:, 0:1], None, ALU.mult
                                        ).then_inc(natt_ready, 1)
                dve.wait_ge(natt_ready, 1)
                dve.wait_ge(xbias_ready, NG + 1)

            def row_pair_step(i, s, stored):
                masked_half(i + 1, 1 - s, 0)
                transposed_lo(i, s, 0)
                transposed_lo(i, s, 1)
                masked_half(i + 1, 1 - s, 1)
                row_maximum(i + 1, 1 - s)
                transposed_lo(i, s, 2)
                transposed_lo(i, s, 3)
                if isinstance(i, int) and i == 0:
                    node_attention()
                finish_row(i, s, stored)

            masked_half(0, 0, 0)
            masked_half(0, 0, 1)
            row_maximum(0, 0)
            dve.wait_ge(vgmax_s, 1)
            nc.vector.tensor_scalar(v_ngmax[:, :], v_gmax[:, :], -1.0, None, ALU.mult).then_inc(vneg_s, 1)
            row_pair_step(0, 0, None)
            row_pair_step(1, 1, None)
            with dve.Fori(1, NT // 2 - 1) as i:
                for s in range(2):
                    row_pair_step(i * 2 + s, s, i * 16)
            row_pair_step(NT - 2, 0, 16 * (NT // 2 - 1))
            for q in range(4):
                transposed_lo(NT - 1, 1, q)
            finish_row(NT - 1, 1, 16 * (NT // 2 - 1))

        @block.tensor
        def _(pe):
            def transpose_group(n):
                tb = 0 if n < NG else 4
                pe.wait_ge(z_ready, n + 1)
                if n == 0:
                    pe.wait_ge(consts_ready, 1)
                if n == NG:
                    pe.wait_ge(xb_free, NG + 1)
                if n >= 1:
                    pe.wait_ge(sthi_ready, n)
                    pe.wait_ge(stlo_ready, n)
                for t in range(GT):
                    for k in range(KD):
                        last = nc.tensor.transpose(ps[:, tb + k, t * P:(t + 1) * P],
                                                   z_rows(n)[:, t, k * P:(k + 1) * P], ident[:, :])
                last.then_inc(tr_done, 1)

            def stage(part, n, cols):
                return lambda k: part[:, n % 2, k, cols]

            transpose_group(0)
            for g in range(NG):
                pe.wait_ge(sthi_ready, g + 1)
                pe.wait_ge(stlo_ready, g + 1)
                if g == 0:
                    pe.wait_ge(wsplit, 1)
                every = slice(0, GN)
                if g >= 2:
                    pe.wait_ge(sl_ready, g - 1)
                three_products(ps[:, 6 + g % 2, :], lambda k: ul_hi[:, k, :], lambda k: ul_lo[:, k, :],
                               stage(stage_hi, g, every), stage(stage_lo, g, every)).then_inc(sl_done, 1)
                for t in range(GT):
                    if t == 2 and g + 1 < NG:
                        transpose_group(g + 1)
                    j = g * GT + t
                    cols = slice(t * P, (t + 1) * P)
                    hi, lo = stage(stage_hi, g, cols), stage(stage_lo, g, cols)
                    if j >= 2:
                        pe.wait_ge(g_lo, j - 1)
                    for c in range(2):
                        last = three_products(ps[:, 2 + 2 * (j % 2) + c, 0:DE], hi, lo, lambda k: w0_hi[:, k, c, :],
                                              lambda k: w0_lo[:, k, c, :])
                    last.then_inc(g_done, 1)

            pe.wait_ge(sl_ready, NG)
            def gcn_quarter(b, q):
                if q == 0:
                    pe.wait_ge(xb_free, b + 1)
                pe.wait_ge(adj_loaded[q], b * 16 + 16)
                for t in (2, 3, 0, 1):
                    if isinstance(b, int) and q == 0 and t == 0:
                        pe.wait_ge(g_lo, NT)
                    for j in range(4 * q, 4 * q + 4):
                        lhs = adj_ring[:, j, t * P:(t + 1) * P]
                        nc.tensor.matmul(ps[:, 4 + t, 0:DX], lhs, ab_hi[:, j, 1, 0:DX], start=(j == 0), stop=False)
                        last = nc.tensor.matmul(ps[:, 4 + t, 0:DX], lhs, ab_lo[:, j, 1, 0:DX], start=False,
                                                stop=(j == NT - 1))
                last.then_inc(adj_pe, 1)

            def attention_pair(b, p):
                if p == 0:
                    pe.wait_ge(xa_free, b + 1)
                pe.wait_ge(elo_ready, b * PAIRS + (EW + p + 1))
                for h in range(2):
                    j = 2 * p + h
                    for t in range(GT):
                        cols = slice(t * P, (t + 1) * P)
                        hi, lo = e_hi[:, p % ER, h, cols], e_lo[:, p % ER, h, cols]
                        nc.tensor.matmul(ps[:, t, 0:DX], hi, ab_hi[:, j, 0, 0:DX], start=(j == 0), stop=False)
                        nc.tensor.matmul(ps[:, t, 0:D], hi, ab_lo[:, j, 0, 0:D], start=False, stop=False)
                        last = nc.tensor.matmul(ps[:, t, 0:DX], lo, ab_hi[:, j, 0, 0:DX], start=False,
                                                stop=(j == NT - 1))
                last.then_inc(e_used, 1)

            pe.wait_ge(g_lo, NT - 2)
            for q in range(4):
                gcn_quarter(0, q)
            pe.wait_ge(ab_ready, 2)
            with pe.Fori(0, NG - 1) as b:
                for p in range(PAIRS):
                    attention_pair(b, p)
                    if p in GCN_AFTER:
                        gcn_quarter(b + 1, GCN_AFTER.index(p))
            for p in range(PAIRS):
                attention_pair(NG - 1, p)
                if p == 6:
                    transpose_group(NG)

            pe.wait_ge(w1_s, 1)
            for g in range(NG):
                n = NG + g
                pe.wait_ge(sthi_ready, n + 1)
                pe.wait_ge(stlo_ready, n + 1)
                every = slice(0, GN)
                for m in range(KD):
                    if g >= 1:
                        pe.wait_ge(h1_lo, (g - 1) * KD + m + 1)
                    rows = slice(m * P, (m + 1) * P)
                    three_products(ps[:, 6 + m, :], lambda k: w1_hi[:, k, rows], lambda k: w1_lo[:, k, rows],
                                   stage(stage_hi, n, every), stage(stage_lo, n, every)).then_inc(h1_done, 1)
                if g < NG - 1:
                    transpose_group(n + 1)
                for t in range(GT):
                    if g == 0 and t == 0:
                        pe.wait_ge(xa_free, NG + 1)
                    if g >= 1:
                        pe.wait_ge(s1_lo, (g - 1) * GT + t + 1)
                    cols = slice(t * P, (t + 1) * P)
                    wide = slice(D, 2 * D + 2)
                    three_products(ps[:, t, 0:DX], stage(stage_hi, n, cols), stage(stage_lo, n, cols),
                                   lambda k: w1_hi[:, k, wide], lambda k: w1_lo[:, k, wide]).then_inc(s1_done, 1)

            def score_half(i, s, h):
                if isinstance(i, int) and i < 2:
                    rows = slice(i * P, (i + 1) * P)
                    lhs_hi, lhs_lo = (lambda k: hh_hi[:, k, rows]), (lambda k: hh_lo[:, k, rows])
                else:
                    lhs_hi, lhs_lo = (lambda k: hs_hi[:, s, k, :]), (lambda k: hs_lo[:, s, k, :])
                if isinstance(i, int) and i == 0:
                    pe.wait_ge(s1_lo, NT - 2 + 2 * h)
                else:
                    pe.wait_ge(em_ready, i * 2 + (h - 1))
                for c in range(2 * h, 2 * h + 2):
                    cols = slice(c * GN, (c + 1) * GN)
                    last = three_products(ps[:, c, :], lhs_hi, lhs_lo, lambda k: hh_hi[:, k, cols],
                                          lambda k: hh_lo[:, k, cols])
                last.then_inc(e_done, 1)

            def transpose_quarter(i, s, q, first):
                if q >= 2 or not first:
                    pe.wait_ge(ptlo_ready, i * 4 + (q - 1))
                for t in range(4):
                    last = nc.tensor.transpose(ps[:, 4 + q % 2, t * P:(t + 1) * P],
                                               em[:, s, (4 * q + t) * P:(4 * q + t + 1) * P], ident[:, :])
                last.then_inc(t_done, 1)

            def row_products(i, s, first):
                if not first:
                    pe.wait_ge(o_ready, i - 1)
                for q in range(4):
                    pe.wait_ge(ptlo_ready, i * 4 + q + 1)
                    for j in range(4 * q, 4 * q + 4):
                        def hi_product():
                            return nc.tensor.matmul(ps[:, 6 + s, :], pt_hi[:, s, j, :], s_hl[:, j, :, :],
                                                    start=(j == 0), stop=(j == NT - 1))
                        if j == 0:
                            hi_product()
                        last = nc.tensor.matmul(ps[:, 6 + s, 0:D], pt_lo[:, s, j, :], s_hl[:, j, 0, :], start=False,
                                                stop=False)
                        if j > 0:
                            last = hi_product()
                last.then_inc(o_done, 1)

            def row_step(i, s, first, first_o):
                if not (isinstance(i, int) and i == 0):
                    pe.wait_ge(hs_ready, i)
                score_half(i + 1, 1 - s, 0)
                pe.wait_ge(p_ready, i + 1)
                transpose_quarter(i, s, 0, first)
                transpose_quarter(i, s, 1, first)
                score_half(i + 1, 1 - s, 1)
                transpose_quarter(i, s, 2, first)
                transpose_quarter(i, s, 3, first)
                row_products(i, s, first_o)

            pe.wait_ge(h1_lo, KD * NG)
            score_half(0, 0, 0)
            score_half(0, 0, 1)
            row_step(0, 0, True, True)
            row_step(1, 1, False, True)
            with pe.Fori(1, NT // 2 - 1) as i:
                for s in range(2):
                    row_step(i * 2 + s, s, False, False)
            row_step(NT - 2, 0, False, False)
            pe.wait_ge(p_ready, NT)
            for q in range(4):
                transpose_quarter(NT - 1, 1, q, False)
            row_products(NT - 1, 1, False)


_INS = ["x", "adj", "adj_t", "L0_gnn_W_sa", "L0_gnn_a_sa", "L0_gnn_W_gcnb", "L0_gnn_b_gcnb", "L0_gnn_Wa", "L0_gnn_ba",
        "L0_gnn_Wb", "L0_gnn_bb", "L1_gnn_weight", "L1_gnn_bias", "L1_gnn_node_w", "L1_gnn_edge_w"]


def kernel(**inputs):
    import numpy as _np
    import concourse.bacc as _bacc
    from concourse import mybir as _mybir
    from concourse.bass_utils import run_bass_kernel_spmd as _run

    nc = _bacc.Bacc("TRN2", target_bir_lowering=False, num_devices=1)
    arrays, args = {}, []
    for name in _INS:
        a = _np.asarray(inputs["adj"]).T if name == "adj_t" else inputs[name]
        a = _np.ascontiguousarray(a)
        arrays[f"in_{name}_dram"] = a
        args.append(nc.dram_tensor(f"in_{name}_dram", a.shape, _mybir.dt.from_np(a.dtype), kind="ExternalInput").ap())
    x = arrays["in_x_dram"]
    args.append(nc.dram_tensor("out_0_dram", x.shape, _mybir.dt.from_np(x.dtype), kind="ExternalOutput").ap())
    build_two_graph_blocks(nc, *args)
    r = _run(nc, [arrays], core_ids=[0])
    return r.results[0]["out_0_dram"]
```
